# Optimizing a Trainium2 kernel written in Bass

```python
import numpy as np
import jax
import jax.numpy as jnp

def _softmax(x, axis=-1):
    return jax.nn.softmax(x, axis=axis)

def _gelu(x):
    return jax.nn.gelu(x, approximate=True)

def _silu(x):
    return jax.nn.silu(x)

def _sigmoid(x):
    return jax.nn.sigmoid(x)

def _layernorm(x, axis=-1, eps=1e-05):
    m = jnp.mean(x, axis=axis, keepdims=True)
    v = jnp.var(x, axis=axis, keepdims=True)
    return (x - m) / jnp.sqrt(v + eps)

def _scatter_add(tgt, idx, src, axis=0):
    return tgt.at[idx].add(src)

def _segment_sum(src, seg, n):
    return jax.ops.segment_sum(src, seg, n)
kernel_name = 'mk_adaln_ffn_d1_seqx_r2_fff9f0'

def setup_inputs(seed: int=0):
    np.random.seed(seed)
    _w = jnp.asarray

    def _rec_inputs():
        import jax
        import jax.numpy as jnp
        _rk = jax.random.key(seed)
        x = -0.0003929 + 0.9999 * jax.random.normal(jax.random.fold_in(_rk, 1), (4, 1024, 512), jnp.float32)
        _lenS = 1024 - jax.random.randint(jax.random.fold_in(_rk, 7), (4,), 0, max(1, 1024 // 4) + 1, jnp.int32)
        _lenS2 = 1024 - jax.random.randint(jax.random.fold_in(_rk, 8), (4,), 0, max(1, 1024 // 4) + 1, jnp.int32)
        cond_256 = -0.0209273 + 1.04763 * jax.random.normal(jax.random.fold_in(_rk, 11), (4, 128), jnp.float32)
        return (x, cond_256)
    x, cond_256 = _rec_inputs()

    def _L0_cond_setup():
        import jax, jax.numpy as jnp
        import numpy as np
        EPS = 1e-08

        def hamilton(q1, q2):
            w1, x1, y1, z1 = (q1[..., i, :] for i in range(4))
            w2, x2, y2, z2 = (q2[..., i, :] for i in range(4))
            w = w1 * w2 - x1 * x2 - y1 * y2 - z1 * z2
            x = w1 * x2 + x1 * w2 + y1 * z2 - z1 * y2
            y = w1 * y2 - x1 * z2 + y1 * w2 + z1 * x2
            z = w1 * z2 + x1 * y2 - y1 * x2 + z1 * w2
            return jnp.stack([w, x, y, z], axis=-2)

        def _normalize(q):
            return q / jnp.sqrt(jnp.sum(q * q, axis=0, keepdims=True) + EPS)
        key = jax.random.key(seed)
        k1, k2, k3, k4 = jax.random.split(key, 4)
        B, T, d_model = (4, 2048, 512)
        quat_dim = d_model // 4
        x = jax.random.normal(k1, (B, T, d_model), dtype=jnp.float32)
        q_left = jax.random.normal(k2, (4, quat_dim), dtype=jnp.float32)
        q_right = jax.random.normal(k3, (4, quat_dim), dtype=jnp.float32)
        spectral_gate = jax.random.uniform(k4, (1, 1, 1, quat_dim), dtype=jnp.float32)
        return {'x': x, 'q_left': q_left, 'q_right': q_right, 'spectral_gate': spectral_gate}
    _L0_cond_all = _L0_cond_setup()
    _L0_cond_in = {k: v for k, v in _L0_cond_all.items() if k in ('q_right', 'spectral_gate')}
    del _L0_cond_all

    def _L0_ffn_setup():
        import jax, jax.numpy as jnp
        import numpy as np
        E = 8
        K = 2
        D = 512
        H = 2048
        CAP_FACTOR = 1.0
        key = jax.random.key(seed)
        ks = jax.random.split(key, 5)
        x = jax.random.normal(ks[0], (4, 1024, D), jnp.float32)
        gate_w = jax.random.normal(ks[1], (E, D), jnp.float32) * 0.02
        fc1_w = jax.random.normal(ks[2], (E, H, D), jnp.float32) * 0.02
        fc1_b = jnp.zeros((E, 1, H), jnp.float32)
        fc2_w = jax.random.normal(ks[3], (E, H, D), jnp.float32) * 0.02
        fc2_b = jnp.zeros((E, 1, D), jnp.float32)
        return {'x': x, 'gate_w': gate_w, 'fc1_w': fc1_w, 'fc1_b': fc1_b, 'fc2_w': fc2_w, 'fc2_b': fc2_b}
    _L0_ffn_all = _L0_ffn_setup()
    _L0_ffn_in = {k: v for k, v in _L0_ffn_all.items() if k in ('gate_w', 'fc1_w', 'fc1_b', 'fc2_w', 'fc2_b')}
    del _L0_ffn_all
    return {'x': x, 'cond_256': cond_256, 'L0_cond_q_right': _L0_cond_in['q_right'], 'L0_cond_spectral_gate': _L0_cond_in['spectral_gate'], 'L0_ffn_gate_w': _L0_ffn_in['gate_w'], 'L0_ffn_fc1_w': _L0_ffn_in['fc1_w'], 'L0_ffn_fc1_b': _L0_ffn_in['fc1_b'], 'L0_ffn_fc2_w': _L0_ffn_in['fc2_w'], 'L0_ffn_fc2_b': _L0_ffn_in['fc2_b']}

def reference(x, cond_256, L0_cond_q_right, L0_cond_spectral_gate, L0_ffn_gate_w, L0_ffn_fc1_w, L0_ffn_fc1_b, L0_ffn_fc2_w, L0_ffn_fc2_b):
    import jax
    import jax.numpy as jnp

    def _L0_cond_ref(x, q_left, q_right, spectral_gate):
        import jax, jax.numpy as jnp
        import numpy as np
        EPS = 1e-08

        def hamilton(q1, q2):
            w1, x1, y1, z1 = (q1[..., i, :] for i in range(4))
            w2, x2, y2, z2 = (q2[..., i, :] for i in range(4))
            w = w1 * w2 - x1 * x2 - y1 * y2 - z1 * z2
            x = w1 * x2 + x1 * w2 + y1 * z2 - z1 * y2
            y = w1 * y2 - x1 * z2 + y1 * w2 + z1 * x2
            z = w1 * z2 + x1 * y2 - y1 * x2 + z1 * w2
            return jnp.stack([w, x, y, z], axis=-2)

        def _normalize(q):
            return q / jnp.sqrt(jnp.sum(q * q, axis=0, keepdims=True) + EPS)
        B, T, d_model = x.shape
        quat_dim = d_model // 4
        x_quat = x.reshape(B, T, 4, quat_dim)
        x_spectral = jnp.fft.fft(x_quat, axis=1)
        x_filtered = jnp.fft.ifft(x_spectral * spectral_gate, axis=1).real.astype(x.dtype)
        q_left_n = _normalize(q_left)
        q_right_n = _normalize(q_right)
        conj_sign = jnp.array([1.0, -1.0, -1.0, -1.0], dtype=x.dtype)[:, None]
        q_right_conj = q_right_n * conj_sign
        x_right = hamilton(x_filtered, q_right_conj)
        x_rotated = hamilton(q_left_n, x_right)
        return x_rotated.reshape(B, T, d_model)

    def _L0_ffn_ref(x, gate_w, fc1_w, fc1_b, fc2_w, fc2_b):
        import jax, jax.numpy as jnp
        import numpy as np
        E = 8
        K = 2
        D = 512
        H = 2048
        CAP_FACTOR = 1.0
        B, S, Dm = x.shape
        xf = x.reshape(-1, Dm)
        N = xf.shape[0]
        cap = int(K * CAP_FACTOR * ((N + E - 1) // E))
        logits = xf @ gate_w.T
        scores = jax.nn.softmax(logits, axis=-1)
        topv, topi = jax.lax.top_k(scores, K)
        gates = topv / jnp.sum(topv, axis=-1, keepdims=True)
        offset = jnp.zeros((E,), jnp.int32)
        locs = []
        for j in range(K):
            mask = jax.nn.one_hot(topi[:, j], E, dtype=jnp.int32)
            loc_in = jnp.cumsum(mask, axis=0) - 1 + offset[None, :]
            locs.append(jnp.take_along_axis(loc_in, topi[:, j:j + 1], axis=1)[:, 0])
            offset = offset + mask.sum(axis=0)
        loc = jnp.stack(locs, axis=1)
        valid = loc < cap
        flat_idx = jnp.where(valid, topi * cap + loc, 0)
        w = valid.astype(xf.dtype)
        disp = jnp.zeros((E * cap, Dm), xf.dtype)
        disp = disp.at[flat_idx.reshape(-1)].add((xf[:, None, :] * w[:, :, None]).reshape(-1, Dm))
        de = disp.reshape(E, cap, Dm)
        h = jax.nn.relu(jnp.einsum('ecd,ehd->ech', de, fc1_w) + fc1_b)
        eo = jnp.einsum('ech,ehd->ecd', h, fc2_w) + fc2_b
        gathered = eo.reshape(E * cap, Dm)[flat_idx]
        out = jnp.sum(gathered * (gates * w)[:, :, None], axis=1)
        return out.reshape(B, S, Dm)
    x = x + _L0_ffn_ref(_L0_cond_ref(x, cond_256, L0_cond_q_right, L0_cond_spectral_gate), L0_ffn_gate_w, L0_ffn_fc1_w, L0_ffn_fc1_b, L0_ffn_fc2_w, L0_ffn_fc2_b)
    return x

_drawn_inputs = setup_inputs


def setup_inputs(seed=0):
    import zlib

    import numpy as np

    out = dict(_drawn_inputs(seed))
    spreads = {'L0_ffn_fc1_b': (0.0, 0.1), 'L0_ffn_fc2_b': (0.0, 0.1)}
    factors = {}
    for name, (base, spread) in spreads.items():
        noise = np.random.default_rng([zlib.crc32(name.encode()), seed]).standard_normal(out[name].shape)
        drawn = base * np.exp(spread * noise) if base else spread * noise
        out[name] = jnp.asarray(drawn.astype(out[name].dtype))
    for name, factor in factors.items():
        out[name] = (out[name] * factor).astype(out[name].dtype)
    return out
```

```python
from contextlib import ExitStack

import concourse.bass as bass
from concourse import mybir

F32 = mybir.dt.float32
F32R = mybir.dt.float32r
I32 = mybir.dt.int32
ACT = mybir.ActivationFunctionType
ALU = mybir.AluOpType
X = mybir.AxisListType.X
ds = bass.ds

P = 128


def program(nc, x, cond, q_right, spectral, gate_w, fc1_w, fc1_b, fc2_w, fc2_b, out):
    B, S, D = x.shape
    E, H, _ = fc1_w.shape
    TOKENS = B * S
    TOPK = 2
    CAP = TOPK * (TOKENS // E)
    Q = D // P
    TJ = TOKENS // P
    HT = H // P
    SLAB = 512
    SB = SLAB // P
    SLABS = CAP // SLAB
    BLOCKS = E * CAP // P
    NS = E * SLABS
    STEPS = SLABS * HT
    AHEAD = 2
    RAW = 2
    HALF = SLAB // 2
    ROT_AT = (3, 6, 9, 12)
    FINISH_AT = (8, 14)
    PRE_AT = (4, 5, 6, 7)
    XC = 4
    XRING = 4
    ROUND = XC * XRING
    ROUNDS = TJ // ROUND
    HOT = 16
    SKIP = 2 * TOKENS

    x_rows = x.rearrange("b s d -> (b s) d")
    x_tiles = x_rows.rearrange("(p j) d -> p j d", j=TJ)
    out_rows = out.rearrange("b s d -> (b s) d")
    out_tiles = out_rows.rearrange("(p j) d -> p j d", j=TJ)
    w1_rows = fc1_w.rearrange("e h d -> (e h) d")
    w2_rows = fc2_w.rearrange("e h d -> (e h) d")
    b2_rows = fc2_b.rearrange("e a d -> (e a) d")
    gates_dram = nc.dram_tensor("gates_dram", [TOKENS * E, 1], F32, kind="Internal").ap()

    ctx = ExitStack()
    with ctx:
        def sb(name, shape, dt=F32, where=ctx):
            return where.enter_context(nc.sbuf_tensor(name, shape, dt))

        def sem(name):
            return ctx.enter_context(nc.semaphore(name))

        ident = sb("ident", [P, P])
        rot = sb("rot", [P, Q, Q])
        b1T = sb("b1T", [P, E * HT])
        gather_row = sb("gather_row", [P, BLOCKS], I32)
        scatter_row = sb("scatter_row", [P, BLOCKS], I32)
        gate_row = sb("gate_row", [P, BLOCKS], I32)
        w1T_hi = sb("w1T_hi", [P, HT, Q, P], F32R)
        w1T_lo = sb("w1T_lo", [P, HT, Q, P], F32R)
        w1_raw = sb("w1_raw", [P, RAW, D])
        w2_raw = sb("w2_raw", [P, RAW, D])

        early = ExitStack()
        x_ring = sb("x_ring", [P, XRING, XC, D], where=early)
        hot_b = sb("hot_b", [P, 2, HOT, P], F32R, where=early)
        hot_q = sb("hot_q", [P, 2, HOT, BLOCKS], F32R, where=early)
        hot_t = sb("hot_t", [P, HOT, BLOCKS], where=early)
        xT = sb("xT", [P, 4, Q, P], where=early)
        small = sb("small", [16, P], where=early)
        gw_nat = sb("gw_nat", [E, D], where=early)
        b1_nat = sb("b1_nat", [E * HT, P], where=early)
        qq = sb("qq", [P, 9], where=early)
        sq = sb("sq", [P, 2, Q], where=early)
        nrm = sb("nrm", [P, 4], where=early)
        qn = sb("qn", [P, 2, Q], where=early)
        neg = sb("neg", [P, 2, Q], where=early)
        Lm = sb("Lm", [P, Q, Q], where=early)
        Rm = sb("Rm", [P, Q, Q], where=early)
        rt = sb("rt", [P, Q, Q], where=early)
        gwT = sb("gwT", [P, Q, E], where=early)
        grot = sb("grot", [P, Q, E], where=early)
        gt = sb("gt", [P, Q, E], where=early)
        iota_i = sb("iota_i", [P, P], I32, where=early)
        iota_f = sb("iota_f", [P, P], where=early)
        id_i = sb("id_i", [P, TJ], I32, where=early)
        id_f = sb("id_f", [P, TJ], where=early)
        first_i = sb("first_i", [P, E], I32, where=early)
        first_f = sb("first_f", [P, E], where=early)
        base_i = sb("base_i", [P, E], I32, where=early)
        base_f = sb("base_f", [P, E], where=early)
        ones = sb("ones", [P, P], where=early)
        before = sb("before", [P, P], where=early)
        carry = sb("carry", [P, TOPK * E, TJ], where=early)
        dl = sb("dl", [P, TJ, E], where=early)
        ex = sb("ex", [P, TJ, E], where=early)
        score = sb("score", [P, TJ, E], where=early)
        wt = sb("wt", [P, TJ, E], where=early)
        gm = sb("gm", [P, TJ, E], where=early)
        st = sb("st", [P, 12, TJ], where=early)
        hot = sb("hot", [P, TOPK, E, TJ], where=early)
        cnt = sb("cnt", [P, TOPK * E, TJ], where=early)
        loc = sb("loc", [P, TOPK * E, TJ], where=early)
        tot = sb("tot", [P, TOPK * E], where=early)
        slot1 = sb("slot1", [P, TOPK, TJ], where=early)
        slot_i = sb("slot_i", [P, TOPK * TJ], I32, where=early)
        q_i = sb("q_i", [P, TOPK * TJ], I32, where=early)
        b_i = sb("b_i", [P, TOPK * TJ], I32, where=early)
        q_f = sb("q_f", [P, TOPK * TJ], where=early)
        b_f = sb("b_f", [P, TOPK * TJ], where=early)
        skip = sb("skip", [P, BLOCKS], where=early)
        gate_f = sb("gate_f", [P, BLOCKS], where=early)
        expert_i = sb("expert_i", [P, BLOCKS], I32, where=early)
        expert_f = sb("expert_f", [P, BLOCKS], where=early)
        early.close()

        w2_hi = sb("w2_hi", [P, HT, D], F32R)
        w2_lo = sb("w2_lo", [P, HT, D], F32R)
        yT_hi = sb("yT_hi", [P, 2, Q, SLAB], F32R)
        yT_lo = sb("yT_lo", [P, 2, Q, SLAB], F32R)
        h_hi = sb("h_hi", [P, 2, SLAB], F32R)
        h_lo = sb("h_lo", [P, 2, SLAB], F32R)
        h_full = sb("h_full", [P, SLAB])
        x_blk = sb("x_blk", [P, 2, D])
        y_half = sb("y_half", [P, Q, HALF])
        rows = sb("rows", [P, SB, D])
        b2_bc = sb("b2_bc", [P, D])
        gate_now = sb("gate_now", [P, SB])
        gather_now = sb("gather_now", [P, 2, SB], I32)
        scatter_now = sb("scatter_now", [P, 2, SB], I32)
        gate_at_now = sb("gate_at_now", [P, 2, SB], I32)
        b1_next = sb("b1_next", [P, HT])
        b1_now = sb("b1_now", [P, HT])

        eo = ctx.enter_context(nc.psum_tensor("eo", [P, SB, D], F32))
        hp = ctx.enter_context(nc.psum_tensor("hp", [P, 2, SLAB], F32))
        wp = ctx.enter_context(nc.psum_tensor("wp", [P, Q, P], F32))
        xp = ctx.enter_context(nc.psum_tensor("xp", [P, 2, HALF], F32))
        logits = hp[:, 0, 0:TJ * E]
        ahead_ps = hp[:, 1, 0:TOPK * E]
        token_ps = hp[:, 0, 0:BLOCKS]
        small_ps = xp[:, 0, 0:9]
        gw_ps = xp[:, 0, 16:16 + Q * E]
        b1_ps = xp[:, 1, 0:E * HT]

        small_in, gw_in, b1_in = sem("small_in"), sem("gw_in"), sem("b1_in")
        x_in = [sem(f"x_in{c}") for c in range(XRING)]
        out_init = [sem(f"out_init{c}") for c in range(XRING)]
        w1_in = [sem(f"w1_in{c}") for c in range(RAW)]
        w2_in = [sem(f"w2_in{c}") for c in range(RAW)]
        consts_ready, pool_chain, now_ready = sem("consts_ready"), sem("pool_chain"), sem("now_ready")
        small_T, small_kept, b1_kept = sem("small_T"), sem("small_kept"), sem("b1_kept")
        squares_ready, norms_ready, grot_ready = sem("squares_ready"), sem("norms_ready"), sem("grot_ready")
        xT_ps, xT_even, xT_odd, xT_used = sem("xT_ps"), sem("xT_even"), sem("xT_odd"), sem("xT_used")
        shifted, exps_ready, counts_ready, ahead_ready = (
            sem("shifted"), sem("exps_ready"), sem("counts_ready"), sem("ahead_ready"))
        gates_ready, gates_stored = sem("gates_ready"), sem("gates_stored")
        hots_ready, hots_used, slots_ready = sem("hots_ready"), sem("hots_used"), sem("slots_ready")
        dve_chain = sem("dve_chain")
        w1_T, w1_hi_ready, w1_ready = sem("w1_T"), sem("w1_hi_ready"), sem("w1_ready")
        w2_hi_ready, w2_ready = sem("w2_hi_ready"), sem("w2_ready")
        blk_in = [sem(f"blk_in{c}") for c in range(2)]
        x_T, rotated, y_hi_ready, y_ready = sem("x_T"), sem("rotated"), sem("y_hi_ready"), sem("y_ready")
        fc1_done, fc2_done = sem("fc1_done"), sem("fc2_done")
        h_hi_ready, h_full_ready, h_ready = sem("h_hi_ready"), sem("h_full_ready"), sem("h_ready")
        rows_in, b2_in, rows_out = sem("rows_in"), sem("b2_in"), sem("rows_out")
        pre_done, sums_ready, b1_taken, b1_found = (
            sem("pre_done"), sem("sums_ready"), sem("b1_taken"), sem("b1_found"))

        def experts(eng, body):
            with eng.Fori(0, E - 1) as e:
                body(e, False)
            body(E - 1, True)

        block = ctx.enter_context(nc.Block())

        @block.sync
        def _(sp):
            sp.dma_start(small[0:Q, :], cond).then_inc(small_in, 16)
            sp.dma_start(small[Q:2 * Q, :], q_right).then_inc(small_in, 16)
            sp.dma_start(small[2 * Q:2 * Q + 1, :], spectral.rearrange("a b c d -> (a b c) d")).then_inc(small_in, 16)
            sp.dma_start(gw_nat[:, :], gate_w).then_inc(gw_in, 16)
            for c in range(ROUNDS * XRING):
                slot = c % XRING
                if c >= XRING:
                    sp.wait_ge(xT_ps, XC * (c - XRING + 1))
                    sp.wait_ge(out_init[slot], 16 * (c // XRING))
                sp.dma_start(x_ring[:, slot, :, :], x_tiles[:, XC * c:XC * (c + 1), :]).then_inc(x_in[slot], 16)
            sp.dma_start(b1_nat[:, :], fc1_b.rearrange("e a (t p) -> (e a t) p", p=P)).then_inc(b1_in, 16)
            for n in range(RAW):
                sp.dma_start(w1_raw[:, n, :], w1_rows[n * P:(n + 1) * P, :]).then_inc(w1_in[n], 16)
                sp.dma_start(w2_raw[:, n, :], w2_rows[n * P:(n + 1) * P, :]).then_inc(w2_in[n], 16)
            with sp.Fori(1, E * HT // RAW) as m:
                for c in range(RAW):
                    sp.wait_ge(w1_T, RAW * m + (c - RAW + 1))
                    sp.dma_start(w1_raw[:, c, :], w1_rows[ds(m * (RAW * P) + c * P, P), :]).then_inc(w1_in[c], 16)
                    sp.wait_ge(w2_ready, RAW * m + (c - RAW + 1))
                    sp.dma_start(w2_raw[:, c, :], w2_rows[ds(m * (RAW * P) + c * P, P), :]).then_inc(w2_in[c], 16)

        @block.gpsimd
        def _(pool):
            chain = [0]

            def link(ins):
                chain[0] += 1
                ins.then_inc(pool_chain, 1)
                pool.wait_ge(pool_chain, chain[0])

            link(pool.memset(ident[:, :], 0.0))
            pool.affine_select(out=ident[:, :], in_=ident[:, :], compare_op=ALU.not_equal, fill=1.0, base=0,
                               pattern=[[-1, P]], channel_multiplier=1).then_inc(consts_ready, 1)
            pool.iota(iota_i[:, :], pattern=[[1, P]], base=0, channel_multiplier=0)
            pool.iota(id_i[:, :], pattern=[[1, TJ]], base=1, channel_multiplier=TJ)
            pool.iota(first_i[:, :], pattern=[[-1, E]], base=E, channel_multiplier=0)
            pool.iota(expert_i[:, :], pattern=[[1, E], [0, BLOCKS // E]], base=0, channel_multiplier=0)
            pool.iota(base_i[:, :], pattern=[[CAP, E]], base=0, channel_multiplier=0).then_inc(consts_ready, 1)
            link(pool.memset(ones[:, :], 1.0))
            link(pool.memset(carry[:, :, :], 1.0))
            pool.memset(carry[:, :, 0:1], 0.0)
            pool.affine_select(out=before[:, :], in_=ones[:, :], compare_op=ALU.is_gt, fill=0.0, base=0,
                               pattern=[[1, P]], channel_multiplier=-1).then_inc(consts_ready, 1)

            pool.wait_ge(gates_ready, 1)
            pool.dma_start(gates_dram.rearrange("(p j e) a -> p j (e a)", j=TJ, e=E), gm[:, :, :]).then_inc(gates_stored, 16)
            pool.wait_ge(slots_ready, 1)

            def take_rows(s, par):
                pool.tensor_copy(gather_now[:, par, :], gather_row[:, ds(SB * s, SB)]).then_inc(now_ready, 1)
                pool.tensor_copy(scatter_now[:, par, :], scatter_row[:, ds(SB * s, SB)]).then_inc(now_ready, 1)
                pool.tensor_copy(gate_at_now[:, par, :], gate_row[:, ds(SB * s, SB)]).then_inc(now_ready, 1)
                pool.wait_ge(now_ready, 3 * (s + 1))
                pool.nop(nofuse=True)

            def gather_x(s, par, u, first=False):
                if not first:
                    pool.wait_ge(x_T, 4 * s + 2 * u)
                    pool.nop(nofuse=True)
                for bb in range(2):
                    b = 2 * u + bb
                    pool.indirect_dma_start(
                        x_blk[:, bb, :], None, x_rows,
                        bass.IndirectOffsetOnAxis(ap=gather_now[:, par, b:b + 1], axis=0)).then_inc(blk_in[bb], 16)

            def gather_rows(par):
                for b in range(SB):
                    pool.indirect_dma_start(
                        rows[:, b, :], None, out_rows,
                        bass.IndirectOffsetOnAxis(ap=gather_now[:, par, b:b + 1], axis=0)).then_inc(rows_in, 16)
                    pool.indirect_dma_start(
                        gate_now[:, b:b + 1], None, gates_dram,
                        bass.IndirectOffsetOnAxis(ap=gate_at_now[:, par, b:b + 1], axis=0)).then_inc(rows_in, 16)

            take_rows(0, 0)
            gather_x(0, 0, 0, first=True)
            gather_x(0, 0, 1)
            pool.dma_start(b2_bc[:, :], b2_rows[0:1, :].partition_broadcast(P)).then_inc(b2_in, 16)
            pool.wait_ge(gates_stored, 16)
            for c in range(XRING):
                pool.wait_ge(out_init[c], 16 * ROUNDS)
            gather_rows(0)

            def expert(e, last):
                for half in range(SLABS):
                    s = e * SLABS + half
                    end = last and half == SLABS - 1
                    if not end:
                        take_rows(s + 1, (half + 1) % 2)
                        gather_x(s + 1, (half + 1) % 2, 0)
                        gather_x(s + 1, (half + 1) % 2, 1)
                    for b in range(SB):
                        pool.wait_ge(sums_ready, SB * (s + 1) + b + 1)
                        pool.nop(nofuse=True)
                        pool.indirect_dma_start(
                            out_rows, bass.IndirectOffsetOnAxis(ap=scatter_now[:, half, b:b + 1], axis=0),
                            rows[:, b, :], None, bounds_check=TOKENS - 1, oob_is_err=False).then_inc(rows_out, 16)
                    pool.wait_ge(rows_out, (s + 1) * (16 * SB))
                    pool.nop(nofuse=True)
                    if not end:
                        if half == SLABS - 1:
                            pool.dma_start(b2_bc[:, :], b2_rows[ds(e + 1, 1), :].partition_broadcast(P)
                                           ).then_inc(b2_in, 16)
                        gather_rows((half + 1) % 2)

            experts(pool, expert)

        @block.scalar
        def _(act):
            act.wait_ge(squares_ready, 1)
            act.activation(nrm[:, 2:4], nrm[:, 0:2], ACT.Sqrt).then_inc(norms_ready, 1)
            with act.Fori(0, ROUNDS) as r:
                for t in range(ROUND):
                    if t % XC == 0:
                        act.wait_ge(x_in[t // XC], 16 * (r + 1))
                        act.dma_start(out_tiles[:, ds(r * ROUND + t, XC), :], x_ring[:, t // XC, :, :]
                                      ).then_inc(out_init[t // XC], 16)
                    if t % 2 == 0:
                        act.wait_ge(xT_ps, r * ROUND + (t + 1))
                        if t >= 4:
                            act.wait_ge(xT_used, r * ROUND + (t - 3))
                        act.activation(xT[:, t % 4, :, :], eo[:, t % 4, :].rearrange("p (q n) -> p q n", q=Q),
                                       ACT.Copy).then_inc(xT_even, 1)
            act.wait_ge(shifted, 1)
            act.activation(ex[:, :, :], dl[:, :, :], ACT.Exp).then_inc(exps_ready, 1)
            act.wait_ge(slots_ready, 1)
            for c in range(XRING):
                act.wait_ge(out_init[c], 16 * ROUNDS)

            def make_tile(e, hh, n, c):
                act.wait_ge(w1_T, n + 1)
                act.activation(w1T_hi[:, hh, :, :], wp[:, :, :], ACT.Copy).then_inc(w1_hi_ready, 1)
                act.wait_ge(w2_in[c], 16 * e * (HT // RAW) + 16 * (hh // RAW + 1))
                act.activation(w2_hi[:, hh, :], w2_raw[:, c, :], ACT.Copy).then_inc(w2_hi_ready, 1)

            def hidden(g, hh, first=0):
                c = hh % 2
                act.wait_ge(fc1_done, g + 1)
                if first == 0:
                    act.wait_ge(fc2_done, g * SB)
                act.activation(h_hi[:, c, :], hp[:, c, :], ACT.Relu, bias=b1_now[:, hh:hh + 1]).then_inc(h_hi_ready, 1)
                if first < 2:
                    act.wait_ge(h_ready, g + 1)
                act.activation(h_full[:, :], hp[:, c, :], ACT.Relu, bias=b1_now[:, hh:hh + 1]).then_inc(h_full_ready, 1)

            def split_y(s, par, u):
                act.wait_ge(rotated, 8 * s + 4 * u + 4)
                act.activation(yT_hi[:, par, :, u * HALF:(u + 1) * HALF], y_half[:, :, :], ACT.Copy
                               ).then_inc(y_hi_ready, 1)

            for n in range(AHEAD):
                make_tile(0, n, n, n)
            for u in range(2):
                split_y(0, 0, u)
            act.wait_ge(b1_kept, 1)
            act.activation(b1_now[:, :], b1T[:, 0:HT], ACT.Copy).then_inc(b1_taken, 1)
            act.wait_ge(b1_taken, 1)
            hidden(0, 0, first=2)

            def expert(e, last):
                for half in range(SLABS):
                    for hh in range(HT):
                        end = last and half == SLABS - 1
                        g = e * STEPS + half * HT + hh
                        if half == 0 and hh + AHEAD < HT:
                            make_tile(e, hh + AHEAD, e * HT + hh + AHEAD, hh % RAW)
                        if half == SLABS - 1 and hh + AHEAD >= HT and not last:
                            make_tile(e + 1, hh + AHEAD - HT, e * HT + hh + AHEAD, hh % RAW)
                        if not (end and hh == HT - 1):
                            if hh == HT - 1 and half == SLABS - 1:
                                act.wait_ge(b1_found, e + 1)
                                act.wait_ge(h_full_ready, g + 1)
                                act.activation(b1_now[:, :], b1_next[:, :], ACT.Copy).then_inc(b1_taken, 1)
                                act.wait_ge(b1_taken, e + 2)
                            hidden(g + 1, (hh + 1) % HT)
                        if half == SLABS - 1 and hh == HT // 2 and not last:
                            act.activation(b1_next[:, :], b1T[:, ds((e + 1) * HT, HT)], ACT.Copy).then_inc(b1_found, 1)
                        if hh in FINISH_AT and not end:
                            split_y(e * SLABS + half + 1, (half + 1) % 2, FINISH_AT.index(hh))

            experts(act, expert)

        @block.vector
        def _(dve):
            chain = [0]

            def link(ins):
                chain[0] += 1
                ins.then_inc(dve_chain, 1)
                dve.wait_ge(dve_chain, chain[0])

            dve.wait_ge(small_T, 1)
            link(dve.tensor_copy(qq[:, :], small_ps))
            link(dve.tensor_tensor(sq[:, :, :].rearrange("p a q -> p (a q)"), qq[:, 0:2 * Q], qq[:, 0:2 * Q], ALU.mult))
            link(dve.tensor_reduce(nrm[:, 0:2], sq[:, :, :], X, ALU.add))
            dve.tensor_scalar(nrm[:, 0:2], nrm[:, 0:2], 1e-8, None, ALU.add).then_inc(squares_ready, 1)
            dve.wait_ge(norms_ready, 1)
            link(dve.reciprocal(nrm[:, 0:2], nrm[:, 2:4]))
            for a in range(2):
                lastop = dve.tensor_scalar(qn[:, a, :], qq[:, a * Q:(a + 1) * Q], nrm[:, a:a + 1], None, ALU.mult)
            link(lastop)
            link(dve.tensor_scalar(qn[:, 1, 1:Q], qn[:, 1, 1:Q], -1.0, None, ALU.mult))
            link(dve.tensor_scalar(neg[:, :, :], qn[:, :, :], -1.0, None, ALU.mult))
            LEFT = [[(0, 1), (1, -1), (2, -1), (3, -1)], [(1, 1), (0, 1), (3, -1), (2, 1)],
                    [(2, 1), (3, 1), (0, 1), (1, -1)], [(3, 1), (2, -1), (1, 1), (0, 1)]]
            RIGHT = [[(0, 1), (1, -1), (2, -1), (3, -1)], [(1, 1), (0, 1), (3, 1), (2, -1)],
                     [(2, 1), (3, -1), (0, 1), (1, 1)], [(3, 1), (2, 1), (1, -1), (0, 1)]]
            for a, (table, dst) in enumerate(((LEFT, Lm), (RIGHT, Rm))):
                for i in range(Q):
                    for j in range(Q):
                        k, sign = table[i][j]
                        lastop = dve.tensor_copy(dst[:, i, j:j + 1], (qn if sign > 0 else neg)[:, a, k:k + 1])
            link(lastop)
            link(dve.tensor_scalar(Rm[:, :, :], Rm[:, :, :], qq[:, 2 * Q:2 * Q + 1], None, ALU.mult))
            for m in range(Q):
                dst = rot if m == 0 else rt
                link(dve.tensor_tensor(dst[:, :, :], Lm[:, :, m:m + 1].to_broadcast([P, Q, Q]),
                                       Rm[:, m:m + 1, :].to_broadcast([P, Q, Q]), ALU.mult))
                if m:
                    link(dve.tensor_tensor(rot[:, :, :], rot[:, :, :], rt[:, :, :], ALU.add))
            link(dve.tensor_copy(gwT[:, :, :].rearrange("p q e -> p (q e)"), gw_ps))
            for i in range(Q):
                dst = grot if i == 0 else gt
                ins = dve.tensor_tensor(dst[:, :, :], gwT[:, i:i + 1, :].to_broadcast([P, Q, E]),
                                        rot[:, i, :].unsqueeze(2).to_broadcast([P, Q, E]), ALU.mult)
                link(ins)
                if i:
                    ins = dve.tensor_tensor(grot[:, :, :], grot[:, :, :], gt[:, :, :], ALU.add)
                    if i < Q - 1:
                        link(ins)
            ins.then_inc(grot_ready, 1)
            dve.wait_ge(consts_ready, 2)
            dve.tensor_copy(iota_f[:, :], iota_i[:, :])
            dve.tensor_copy(id_f[:, :], id_i[:, :]).then_inc(h_ready, 1)
            dve.tensor_copy(first_f[:, :], first_i[:, :])
            dve.tensor_copy(expert_f[:, :], expert_i[:, :])
            link(dve.tensor_copy(base_f[:, :], base_i[:, :]))

            with dve.Fori(0, ROUNDS) as r:
                for t in range(1, ROUND, 2):
                    dve.wait_ge(xT_ps, r * ROUND + (t + 1))
                    if t >= 4:
                        dve.wait_ge(xT_used, r * ROUND + (t - 3))
                    dve.tensor_copy(xT[:, t % 4, :, :], eo[:, t % 4, :].rearrange("p (q n) -> p q n", q=Q)
                                    ).then_inc(xT_odd, 1)

            def per_e(ap):
                return ap.unsqueeze(2).to_broadcast([P, TJ, E])

            lg = logits.rearrange("p (j e) -> p j e", e=E)
            mx, sm, v1, v2, w1m, w2m, gs, g1, g2, e1 = (st[:, k, :] for k in range(10))
            dve.wait_ge(xT_used, TJ)
            link(dve.reduce_max(mx, lg, X))
            dve.tensor_tensor(dl[:, :, :], lg, per_e(mx), ALU.subtract).then_inc(shifted, 1)
            dve.wait_ge(exps_ready, 1)
            link(dve.reduce_sum(sm, ex[:, :, :], X))
            link(dve.reciprocal(sm, sm))
            link(dve.tensor_tensor(score[:, :, :], ex[:, :, :], per_e(sm), ALU.mult))
            first_bc = first_f[:, :].unsqueeze(1).to_broadcast([P, TJ, E])
            for k, (v, w) in enumerate(((v1, w1m), (v2, w2m))):
                hot_k = hot[:, k, :, :].rearrange("p e j -> p j e")
                link(dve.reduce_max(v, score[:, :, :], X))
                link(dve.tensor_tensor(wt[:, :, :], score[:, :, :], per_e(v), ALU.is_equal))
                link(dve.tensor_tensor(wt[:, :, :], wt[:, :, :], first_bc, ALU.mult))
                link(dve.reduce_max(w, wt[:, :, :], X))
                link(dve.tensor_tensor(hot_k, wt[:, :, :], per_e(w), ALU.is_equal))
                if k == 0:
                    link(dve.scalar_tensor_tensor(score[:, :, :], hot_k, -2.0, score[:, :, :], ALU.mult, ALU.add))
            dve.wait_ge(consts_ready, 3)
            cnt2 = cnt[:, :, :].rearrange("p k j -> p (k j)")
            link(dve.tensor_tensor_scan(cnt2, carry[:, :, :].rearrange("p k j -> p (k j)"),
                                        hot[:, :, :, :].rearrange("p k e j -> p (k e j)"), 0.0, ALU.mult, ALU.add))
            dve.tensor_copy(tot[:, :], cnt[:, :, TJ - 1]).then_inc(counts_ready, 1)
            dve.wait_ge(ahead_ready, 1)
            ke = [P, TOPK * E, TJ]
            hot3 = hot[:, :, :, :].rearrange("p k e j -> p (k e) j")
            link(dve.tensor_tensor(cnt[:, :, :], cnt[:, :, :], ahead_ps.unsqueeze(2).to_broadcast(ke), ALU.add))
            link(dve.scalar_tensor_tensor(loc[:, :, :], cnt[:, :, :], float(CAP), hot3, ALU.is_le, ALU.mult))
            for k in range(TOPK):
                part = cnt[:, k * E:(k + 1) * E, :]
                ins = dve.tensor_tensor(part, part, base_f[:, :].unsqueeze(2).to_broadcast([P, E, TJ]), ALU.add)
            link(ins)
            link(dve.tensor_tensor(loc[:, :, :], loc[:, :, :], cnt[:, :, :], ALU.mult))
            link(dve.reduce_sum(slot1[:, :, :], loc[:, :, :].rearrange("p (k e) j -> p k j e", k=TOPK), X))
            link(dve.tensor_scalar(slot_i[:, :], slot1[:, :, :].rearrange("p k j -> p (k j)"), -1.0, None, ALU.add))
            dve.tensor_scalar(q_i[:, :], slot_i[:, :], 7, None, ALU.arith_shift_right)
            link(dve.tensor_scalar(b_i[:, :], slot_i[:, :], P - 1, None, ALU.bitwise_and))
            dve.tensor_copy(q_f[:, :], q_i[:, :]).then_inc(sums_ready, SB)
            link(dve.tensor_copy(b_f[:, :], b_i[:, :]))
            for c in range(TOPK * TJ // HOT):
                if c >= 2:
                    dve.wait_ge(hots_used, c - 1)
                kj = slice(c * HOT, (c + 1) * HOT)
                j = slice(c * HOT % TJ, c * HOT % TJ + HOT)
                dve.tensor_tensor(hot_b[:, c % 2, :, :], iota_f[:, :].unsqueeze(1).to_broadcast([P, HOT, P]),
                                  b_f[:, kj].unsqueeze(2).to_broadcast([P, HOT, P]), ALU.is_equal)
                if c:
                    dve.wait_ge(hots_ready, c)
                link(dve.tensor_tensor(hot_t[:, :, :], iota_f[:, 0:BLOCKS].unsqueeze(1).to_broadcast([P, HOT, BLOCKS]),
                                       q_f[:, kj].unsqueeze(2).to_broadcast([P, HOT, BLOCKS]), ALU.is_equal))
                dve.tensor_tensor(hot_q[:, c % 2, :, :], hot_t[:, :, :],
                                  id_f[:, j].unsqueeze(2).to_broadcast([P, HOT, BLOCKS]), ALU.mult
                                  ).then_inc(hots_ready, 1)
            link(dve.tensor_tensor(gs, v1, v2, ALU.add))
            link(dve.reciprocal(gs, gs))
            dve.tensor_tensor(g1, v1, gs, ALU.mult)
            link(dve.tensor_tensor(g2, v2, gs, ALU.mult))
            dve.tensor_tensor(gm[:, :, :], hot[:, 0, :, :].rearrange("p e j -> p j e"), per_e(g1), ALU.mult)
            link(dve.tensor_tensor(wt[:, :, :], hot[:, 1, :, :].rearrange("p e j -> p j e"), per_e(g2), ALU.mult))
            dve.tensor_tensor(gm[:, :, :], gm[:, :, :], wt[:, :, :], ALU.add).then_inc(gates_ready, 1)
            dve.wait_ge(hots_used, TOPK * TJ // HOT)
            dve.tensor_scalar(gather_row[:, :], token_ps, -1.0, 0.0, ALU.add, ALU.max)
            dve.tensor_scalar(gate_f[:, :], token_ps, -1.0, 0.0, ALU.add, ALU.max)
            link(dve.tensor_scalar(skip[:, :], token_ps, 0.0, float(SKIP), ALU.is_equal, ALU.mult))
            dve.scalar_tensor_tensor(gate_row[:, :], gate_f[:, :], float(E), expert_f[:, :], ALU.mult, ALU.add)
            dve.scalar_tensor_tensor(scatter_row[:, :], token_ps, -1.0, skip[:, :], ALU.add, ALU.add
                                     ).then_inc(slots_ready, 1)
            dve.wait_ge(small_kept, 1)
            dve.tensor_copy(b1T[:, :], b1_ps).then_inc(b1_kept, 1)

            def make_tile(hh, n, c):
                dve.wait_ge(w1_hi_ready, n + 1)
                dve.tensor_tensor(w1T_lo[:, hh, :, :], wp[:, :, :], w1T_hi[:, hh, :, :].bitcast(F32), ALU.subtract
                                  ).then_inc(w1_ready, 1)
                dve.wait_ge(w2_hi_ready, n + 1)
                dve.tensor_tensor(w2_lo[:, hh, :], w2_raw[:, c, :], w2_hi[:, hh, :].bitcast(F32), ALU.subtract
                                  ).then_inc(w2_ready, 1)

            def hidden_low(g, c):
                dve.wait_ge(h_full_ready, g + 1)
                dve.tensor_tensor(h_lo[:, c, :], h_full[:, :], h_hi[:, c, :].bitcast(F32), ALU.subtract
                                  ).then_inc(h_ready, 1)

            def rotate(s, k, jj):
                j = 2 * (k % 2) + jj
                if jj == 0:
                    dve.wait_ge(x_T, 4 * s + k + 1)
                for i in range(Q):
                    if j == 0:
                        if i == 0:
                            dve.wait_ge(y_ready, 2 * s + k // 2)
                        ins = dve.tensor_scalar(y_half[:, i, :], xp[:, jj, :], rot[:, i, j:j + 1], None, ALU.mult)
                    else:
                        if i == 0:
                            dve.wait_ge(rotated, 8 * s + 2 * k + jj)
                        ins = dve.scalar_tensor_tensor(y_half[:, i, :], xp[:, jj, :], rot[:, i, j:j + 1],
                                                       y_half[:, i, :], ALU.mult, ALU.add)
                ins.then_inc(rotated, 1)

            def split_y(s, par, u):
                dve.wait_ge(y_hi_ready, 2 * s + u + 1)
                dst = slice(u * HALF, (u + 1) * HALF)
                dve.tensor_tensor(yT_lo[:, par, :, dst], y_half[:, :, :], yT_hi[:, par, :, dst].bitcast(F32),
                                  ALU.subtract).then_inc(y_ready, 1)

            for n in range(AHEAD):
                make_tile(n, n, n)
            for u in range(2):
                for k in (2 * u, 2 * u + 1):
                    for jj in range(2):
                        rotate(0, k, jj)
                split_y(0, 0, u)
            hidden_low(0, 0)

            def expert(e, last):
                for half in range(SLABS):
                    s = e * SLABS + half
                    end = last and half == SLABS - 1
                    for hh in range(HT):
                        g = e * STEPS + half * HT + hh
                        if half == 0 and hh + AHEAD < HT:
                            make_tile(hh + AHEAD, e * HT + hh + AHEAD, hh % RAW)
                        if half == SLABS - 1 and hh + AHEAD >= HT and not last:
                            make_tile(hh + AHEAD - HT, e * HT + hh + AHEAD, hh % RAW)
                        if not end:
                            for k, at in enumerate(ROT_AT):
                                if hh in (at, at + 1):
                                    rotate(s + 1, k, hh - at)
                            if hh in FINISH_AT:
                                split_y(s + 1, (half + 1) % 2, FINISH_AT.index(hh))
                        if hh in PRE_AT:
                            b = PRE_AT.index(hh)
                            if b == 0:
                                dve.wait_ge(rows_in, (s + 1) * (32 * SB))
                                dve.wait_ge(b2_in, 16 * (e + 1))
                            dve.scalar_tensor_tensor(rows[:, b, :], b2_bc[:, :], gate_now[:, b:b + 1], rows[:, b, :],
                                                     ALU.mult, ALU.add).then_inc(pre_done, 1)
                        if not (end and hh == HT - 1):
                            hidden_low(g + 1, (hh + 1) % 2)
                        if hh == HT - 1:
                            for b in range(SB):
                                dve.wait_ge(fc2_done, (g + 1) * SB + b + 1)
                                dve.wait_ge(pre_done, SB * s + b + 1)
                                dve.scalar_tensor_tensor(rows[:, b, :], eo[:, b, :], gate_now[:, b:b + 1],
                                                         rows[:, b, :], ALU.mult, ALU.add).then_inc(sums_ready, 1)

            experts(dve, expert)

        @block.tensor
        def _(pe):
            pe.wait_ge(consts_ready, 1)
            pe.wait_ge(small_in, 48)
            pe.wait_ge(gw_in, 16)
            pe.transpose(small_ps, small[0:9, :], ident[0:9, 0:9]).then_inc(fc2_done, SB)
            for q in range(Q):
                ins = pe.transpose(gw_ps[:, q * E:(q + 1) * E], gw_nat[:, q * P:(q + 1) * P], ident[0:E, 0:E])
            ins.then_inc(small_T, 1)

            def take_logits(r, t):
                if t % 2 == 0:
                    pe.wait_ge(xT_even, r * (ROUND // 2) + (t // 2 + 1))
                else:
                    pe.wait_ge(xT_odd, r * (ROUND // 2) + (t // 2 + 1))
                for q in range(Q):
                    ins = pe.matmul(logits[:, ds(r * (ROUND * E) + t * E, E)], xT[:, t % 4, q, :], grot[:, q, :],
                                    start=(q == 0), stop=(q == Q - 1))
                ins.then_inc(xT_used, 1)

            with pe.Fori(0, ROUNDS) as r:
                for t in range(ROUND):
                    if t % XC == 0:
                        pe.wait_ge(x_in[t // XC], 16 * (r + 1))
                    for q in range(Q):
                        ins = pe.transpose(eo[:, t % 4, q * P:(q + 1) * P],
                                           x_ring[:, t // XC, t % XC, q * P:(q + 1) * P], ident[:, :])
                    ins.then_inc(xT_ps, 1)
                    if t == 2:
                        pe.wait_ge(grot_ready, 1)
                    if t >= 2:
                        take_logits(r, t - 2)
                take_logits(r, ROUND - 2)
                take_logits(r, ROUND - 1)

            pe.wait_ge(b1_in, 16)
            pe.wait_ge(consts_ready, 3)
            pe.wait_ge(counts_ready, 1)
            pe.matmul(ahead_ps, before[:, :], tot[:, :], start=True, stop=False)
            pe.matmul(ahead_ps[:, E:2 * E], ones[:, :], tot[:, 0:E], start=False, stop=True).then_inc(ahead_ready, 1)
            pe.transpose(b1_ps, b1_nat[:, :], ident[:, :]).then_inc(small_kept, 1)

            def make_tile(e, hh, n, c):
                pe.wait_ge(w1_in[c], 16 * e * (HT // RAW) + 16 * (hh // RAW + 1))
                pe.wait_ge(w1_ready, n)
                for q in range(Q):
                    ins = pe.transpose(wp[:, q, :], w1_raw[:, c, q * P:(q + 1) * P], ident[:, :])
                ins.then_inc(w1_T, 1)

            def transpose_x(s, k, first=False):
                if k % 2 == 0:
                    for bb in range(2):
                        pe.wait_ge(blk_in[bb], 32 * s + 16 * (k // 2 + 1))
                if not first:
                    pe.wait_ge(rotated, 8 * s + 2 * k)
                for jj in range(2):
                    for bb in range(2):
                        j = 2 * (k % 2) + jj
                        ins = pe.transpose(xp[:, jj, bb * P:(bb + 1) * P], x_blk[:, bb, j * P:(j + 1) * P], ident[:, :])
                ins.then_inc(x_T, 1)

            def fc1(g, tile, hh, par, first=False):
                pe.wait_ge(w1_ready, tile + 1)
                if not first:
                    pe.wait_ge(h_ready, g)
                bank = hp[:, hh % 2, :]
                for q in range(Q):
                    pe.matmul(bank, w1T_hi[:, hh, q, :], yT_hi[:, par, q, :], start=(q == 0), stop=False)
                    pe.matmul(bank, w1T_hi[:, hh, q, :], yT_lo[:, par, q, :], start=False, stop=False)
                    ins = pe.matmul(bank, w1T_lo[:, hh, q, :], yT_hi[:, par, q, :], start=False, stop=(q == Q - 1))
                ins.then_inc(fc1_done, 1)

            def fc2(e, g, s, hh, c):
                pe.wait_ge(w2_ready, e * HT + hh + 1)
                pe.wait_ge(h_hi_ready, g + 1)
                for b in range(SB):
                    if hh == 0:
                        pe.wait_ge(sums_ready, SB * s + (b + 1))
                    blk = slice(b * P, (b + 1) * P)
                    pe.matmul(eo[:, b, :], h_hi[:, c, blk], w2_hi[:, hh, :], start=(hh == 0), stop=False)
                    pe.matmul(eo[:, b, :], h_hi[:, c, blk], w2_lo[:, hh, :], start=False, stop=False)
                pe.wait_ge(h_ready, g + 2)
                for b in range(SB):
                    blk = slice(b * P, (b + 1) * P)
                    pe.matmul(eo[:, b, :], h_lo[:, c, blk], w2_hi[:, hh, :], start=False, stop=(hh == HT - 1)
                              ).then_inc(fc2_done, 1)

            make_tile(0, 0, 0, 0)
            for c in range(TOPK * TJ // HOT):
                pe.wait_ge(hots_ready, c + 1)
                for i in range(HOT):
                    ins = pe.matmul(token_ps, hot_b[:, c % 2, i, :], hot_q[:, c % 2, i, :],
                                    start=(c == 0 and i == 0), stop=(c == TOPK * TJ // HOT - 1 and i == HOT - 1))
                ins.then_inc(hots_used, 1)
            make_tile(0, 1, 1, 1)
            pe.wait_ge(b1_kept, 1)
            for k in range(4):
                transpose_x(0, k, first=(k == 0))
            pe.wait_ge(y_ready, 2)
            fc1(0, 0, 0, 0, first=True)

            def expert(e, last):
                for half in range(SLABS):
                    s = e * SLABS + half
                    end = last and half == SLABS - 1
                    for hh in range(HT):
                        g = e * STEPS + half * HT + hh
                        if half == 0 and hh + AHEAD < HT:
                            make_tile(e, hh + AHEAD, e * HT + hh + AHEAD, hh % RAW)
                        if half == SLABS - 1 and hh + AHEAD >= HT and not last:
                            make_tile(e + 1, hh + AHEAD - HT, e * HT + hh + AHEAD, hh % RAW)
                        if hh in ROT_AT and not end:
                            transpose_x(s + 1, ROT_AT.index(hh))
                        if hh < HT - 1:
                            fc1(g + 1, e * HT + hh + 1, hh + 1, half)
                        elif not end:
                            pe.wait_ge(y_ready, 2 * (s + 2))
                            fc1(g + 1, e * HT + (HT if half == SLABS - 1 else 0), 0, (half + 1) % 2)
                        fc2(e, g, s, hh, hh % 2)

            experts(pe, expert)


_INS = ['x', 'cond_256', 'L0_cond_q_right', 'L0_cond_spectral_gate', 'L0_ffn_gate_w', 'L0_ffn_fc1_w',
        'L0_ffn_fc1_b', 'L0_ffn_fc2_w', 'L0_ffn_fc2_b']


def kernel(**inputs):
    import numpy as _np
    import concourse.bacc as _bacc
    from concourse import mybir as _mybir
    from concourse.bass_utils import run_bass_kernel_spmd as _run

    nc = _bacc.Bacc("TRN2", target_bir_lowering=False, num_devices=1)
    arrays, args = {}, []
    for name in _INS:
        a = _np.ascontiguousarray(inputs[name])
        arrays[f"in_{name}"] = a
        args.append(nc.dram_tensor(f"in_{name}", a.shape, _mybir.dt.from_np(a.dtype), kind="ExternalInput").ap())
    shape = tuple(inputs["x"].shape)
    args.append(nc.dram_tensor("out_0", shape, _mybir.dt.float32, kind="ExternalOutput").ap())
    program(nc, *args)
    r = _run(nc, [arrays], core_ids=[0])
    return r.results[0]["out_0"]
```

```python
from contextlib import ExitStack

import concourse.bass as bass
from concourse import mybir

F32 = mybir.dt.float32
F32R = mybir.dt.float32r
I32 = mybir.dt.int32
BF16 = mybir.dt.bfloat16
ACT = mybir.ActivationFunctionType
ALU = mybir.AluOpType
X = mybir.AxisListType.X
ds = bass.ds

P = 128


def program(nc, x, cond, q_right, spectral, gate_w, fc1_w, fc1_b, fc2_w, fc2_b, out):
    B, S, D = x.shape
    E, H, _ = fc1_w.shape
    TOKENS = B * S
    TOPK = 2
    CAP = TOPK * (TOKENS // E)
    Q = D // P
    TJ = TOKENS // P
    HT = H // P
    SLAB = 512
    SB = SLAB // P
    SLABS = CAP // SLAB
    BLOCKS = E * CAP // P
    NS = E * SLABS
    STEPS = SLABS * HT
    AHEAD = 2
    RAW = 2
    HALF = SLAB // 2
    ROT_AT = (4, 6, 9, 11)
    FINISH_AT = (8, 13)
    PRE_AT = (7, 10, 12, 14)
    XC = 4
    CHUNKS = TJ // XC
    UNITS = CHUNKS * Q
    BLK = 32
    W1_DMAS = P // BLK
    SKIP = 2 * TOKENS

    x_rows = x.rearrange("b s d -> (b s) d")
    x_tiles = x_rows.rearrange("(p j) d -> p j d", j=TJ)
    out_rows = out.rearrange("b s d -> (b s) d")
    out_tiles = out_rows.rearrange("(p j) d -> p j d", j=TJ)
    w1_rows = fc1_w.rearrange("e h d -> (e h) d")
    w2_rows = fc2_w.rearrange("e h d -> (e h) d")
    b2_rows = fc2_b.rearrange("e a d -> (e a) d")
    gates_dram = nc.dram_tensor("gates_dram", [TOKENS * E, 1], F32, kind="Internal").ap()

    ctx = ExitStack()
    with ctx:
        def sb(name, shape, dt=F32, where=ctx):
            return where.enter_context(nc.sbuf_tensor(name, shape, dt))

        def sem(name):
            return ctx.enter_context(nc.semaphore(name))

        ident = sb("ident", [P, P])
        rot = sb("rot", [P, Q, Q])
        b1T = sb("b1T", [P, E * HT])
        gather_row = sb("gather_row", [P, BLOCKS], I32)
        scatter_row = sb("scatter_row", [P, BLOCKS], I32)
        gate_row = sb("gate_row", [P, BLOCKS], I32)
        w1T_hi = sb("w1T_hi", [P, HT, Q, P], F32R)
        w1T_lo = sb("w1T_lo", [P, HT, Q, P], F32R)
        w1_raw = sb("w1_raw", [P, RAW, D])
        w2_raw = sb("w2_raw", [P, RAW, D])
        w1_turned = sb("w1_turned", [P, 2, Q, P])

        early = ExitStack()
        x_all = sb("x_all", [P, TJ, D], where=early)
        value = sb("value", [P, P, TJ], BF16, where=early)
        hot_b = sb("hot_b", [P, TOPK, P, TJ], BF16, where=early)
        transposing = ExitStack()
        xT_hi = sb("xT_hi", [P, 2, XC * P], F32R, where=transposing)
        xT_lo = sb("xT_lo", [P, 2, XC * P], F32R, where=transposing)
        logitsT = sb("logitsT", [2 * E, 2, XC * P], where=transposing)
        transposing.close()
        hot_q = sb("hot_q", [P, TOPK, 2, BLOCKS, TJ], BF16, where=early)
        small = sb("small", [16, P], where=early)
        gw_nat = sb("gw_nat", [E, D], where=early)
        b1_nat = sb("b1_nat", [E * HT, P], where=early)
        qq = sb("qq", [P, 9], where=early)
        sq = sb("sq", [P, 2, Q], where=early)
        nrm = sb("nrm", [P, 4], where=early)
        qn = sb("qn", [P, 2, Q], where=early)
        neg = sb("neg", [P, 2, Q], where=early)
        Lm = sb("Lm", [P, Q, Q], where=early)
        Rm = sb("Rm", [P, Q, Q], where=early)
        rt = sb("rt", [P, Q, Q], where=early)
        gwT = sb("gwT", [P, Q, E], where=early)
        grot = sb("grot", [P, Q, E], where=early)
        gt = sb("gt", [P, Q, E], where=early)
        grot_hl = sb("grot_hl", [P, Q, 2 * E], F32R, where=early)
        j1 = sb("j1", [P, TJ], BF16, where=early)
        part_i = sb("part_i", [P, 1], I32, where=early)
        part_f = sb("part_f", [P, 1], where=early)
        lg_low = sb("lg_low", [P, TJ, E], where=early)
        lg = sb("lg", [P, TJ, E], where=early)
        first_i = sb("first_i", [P, E], I32, where=early)
        first_f = sb("first_f", [P, E], where=early)
        base_i = sb("base_i", [P, E], I32, where=early)
        base_f = sb("base_f", [P, E], where=early)
        ones = sb("ones", [P, P], where=early)
        before = sb("before", [P, P], where=early)
        carry = sb("carry", [P, TOPK * E, TJ], where=early)
        dl = sb("dl", [P, TJ, E], where=early)
        ex = sb("ex", [P, TJ, E], where=early)
        score = sb("score", [P, TJ, E], where=early)
        wt = sb("wt", [P, TJ, E], where=early)
        gm = sb("gm", [P, TJ, E], where=early)
        st = sb("st", [P, 12, TJ], where=early)
        hot = sb("hot", [P, TOPK, E, TJ], where=early)
        cnt = sb("cnt", [P, TOPK * E, TJ], where=early)
        loc = sb("loc", [P, TOPK * E, TJ], where=early)
        tot = sb("tot", [P, TOPK * E], where=early)
        slot1 = sb("slot1", [P, TOPK, TJ], where=early)
        slot_i = sb("slot_i", [P, TOPK * TJ], I32, where=early)
        q_i = sb("q_i", [P, TOPK * TJ], I32, where=early)
        b_i = sb("b_i", [P, TOPK * TJ], I32, where=early)
        q_f = sb("q_f", [P, TOPK, TJ], BF16, where=early)
        b_f = sb("b_f", [P, TOPK, TJ], BF16, where=early)
        token1 = sb("token1", [P, BLOCKS], where=early)
        j_part = sb("j_part", [P, BLOCKS], where=early)
        skip = sb("skip", [P, BLOCKS], where=early)
        gate_f = sb("gate_f", [P, BLOCKS], where=early)
        expert_i = sb("expert_i", [P, BLOCKS], I32, where=early)
        expert_f = sb("expert_f", [P, BLOCKS], where=early)
        early.close()

        w2_hi = sb("w2_hi", [P, HT, D], F32R)
        w2_lo = sb("w2_lo", [P, HT, D], F32R)
        yT_hi = sb("yT_hi", [P, 2, Q, SLAB], F32R)
        yT_lo = sb("yT_lo", [P, 2, Q, SLAB], F32R)
        h_hi = sb("h_hi", [P, 2, SLAB], F32R)
        h_lo = sb("h_lo", [P, 2, SLAB], F32R)
        h_full = sb("h_full", [P, SLAB])
        x_blk = sb("x_blk", [P, 2, D])
        y_half = sb("y_half", [P, Q, HALF])
        rows = sb("rows", [P, SB, D])
        b2_bc = sb("b2_bc", [P, D])
        gate_now = sb("gate_now", [P, SB])
        gather_now = sb("gather_now", [P, 2, SB], I32)
        scatter_now = sb("scatter_now", [P, 2, SB], I32)
        gate_at_now = sb("gate_at_now", [P, 2, SB], I32)
        b1_next = sb("b1_next", [P, HT])
        b1_now = sb("b1_now", [P, HT])

        eo = ctx.enter_context(nc.psum_tensor("eo", [P, SB, D], F32))
        hp = ctx.enter_context(nc.psum_tensor("hp", [P, 2, SLAB], F32))
        wp = ctx.enter_context(nc.psum_tensor("wp", [P, Q, P], F32))
        xp = ctx.enter_context(nc.psum_tensor("xp", [P, 2, HALF], F32))
        xp_all = xp[:, :, :].rearrange("p a n -> p (a n)")
        logits_hl = xp_all.rearrange("p (j a e) -> p j a e", a=2, e=E)
        ahead_ps = hp[:, 1, 0:TOPK * E]
        token_ps = hp[:, 0, 0:2 * BLOCKS].rearrange("p (a q) -> p a q", a=2)
        wp_all = wp[:, :, :].rearrange("p q n -> p (q n)")
        small_ps = wp_all[:, 0:9]
        gw_ps = wp_all[:, 16:16 + Q * E]
        b1_ps = wp_all[:, P:P + E * HT]
        y_sum = y_half[:, :, :].rearrange("p q n -> p (q n)").rearrange("p (a n) -> p a n", a=2)

        small_in, gw_in, b1_in = sem("small_in"), sem("gw_in"), sem("b1_in")
        x_in = [sem(f"x_in{c}") for c in range(CHUNKS)]
        x0_in = [sem(f"x0_in{b}") for b in range(SB)]
        out_init = sem("out_init")
        w1_in = [sem(f"w1_in{c}") for c in range(RAW)]
        w2_in = [sem(f"w2_in{c}") for c in range(RAW)]
        consts_ready, pool_chain, now_ready = sem("consts_ready"), sem("pool_chain"), sem("now_ready")
        small_T, b1_kept = sem("small_T"), sem("b1_kept")
        squares_ready, norms_ready, grot_ready = sem("squares_ready"), sem("norms_ready"), sem("grot_ready")
        xT_ps, xT_hi_ready, xT_ready, xT_used = sem("xT_ps"), sem("xT_hi_ready"), sem("xT_ready"), sem("xT_used")
        logitsT_kept, logits_T = sem("logitsT_kept"), sem("logits_T")
        y0_begun = sem("y0_begun")
        shifted, exps_ready, counts_ready, ahead_ready = (
            sem("shifted"), sem("exps_ready"), sem("counts_ready"), sem("ahead_ready"))
        gates_ready, gates_stored = sem("gates_ready"), sem("gates_stored")
        hots_ready, hots_used, slots_ready = sem("hots_ready"), sem("hots_used"), sem("slots_ready")
        dve_chain = sem("dve_chain")
        w1_T, w1_hi_ready, w1_ready = sem("w1_T"), sem("w1_hi_ready"), sem("w1_ready")
        w2_hi_ready, w2_ready = sem("w2_hi_ready"), sem("w2_ready")
        blk_in = [sem(f"blk_in{c}") for c in range(2)]
        x_T, rotated, y_hi_ready, y_ready = sem("x_T"), sem("rotated"), sem("y_hi_ready"), sem("y_ready")
        fc1_done, fc2_done = sem("fc1_done"), sem("fc2_done")
        h_hi_ready, h_full_ready, h_ready = sem("h_hi_ready"), sem("h_full_ready"), sem("h_ready")
        rows_in, b2_in, rows_out = sem("rows_in"), sem("b2_in"), sem("rows_out")
        pre_done, sums_ready, b1_taken, b1_found = (
            sem("pre_done"), sem("sums_ready"), sem("b1_taken"), sem("b1_found"))

        def experts(eng, body):
            with eng.Fori(0, E - 1) as e:
                body(e, False)
            body(E - 1, True)

        block = ctx.enter_context(nc.Block())

        @block.sync
        def _(sp):
            sp.dma_start(small[0:Q, :], cond).then_inc(small_in, 16)
            sp.dma_start(small[Q:2 * Q, :], q_right).then_inc(small_in, 16)
            sp.dma_start(small[2 * Q:2 * Q + 1, :], spectral.rearrange("a b c d -> (a b c) d")).then_inc(small_in, 16)
            sp.dma_start(gw_nat[:, :], gate_w).then_inc(gw_in, 16)
            sp.dma_start(b1_nat[:, :], fc1_b.rearrange("e a (t p) -> (e a t) p", p=P)).then_inc(b1_in, 16)
            for c in range(CHUNKS):
                tiles = slice(XC * c, XC * (c + 1))
                sp.dma_start(x_all[:, tiles, :], x_tiles[:, tiles, :]).then_inc(x_in[c], 16)
            def load_w1(row, c):
                tile = w1_rows[ds(row, P), :].rearrange("(hq r) (k dq c) -> dq r k hq c", r=BLK, k=Q, c=BLK)
                for dq in range(P // BLK):
                    part = w1_raw[dq * BLK:(dq + 1) * BLK, c, :].rearrange("r (k hq c) -> r k hq c", k=Q, c=BLK)
                    sp.dma_start(part, tile[dq]).then_inc(w1_in[c], 16)

            for n in range(RAW):
                load_w1(n * P, n)
                sp.dma_start(w2_raw[:, n, :], w2_rows[n * P:(n + 1) * P, :]).then_inc(w2_in[n], 16)
            for c in range(CHUNKS):
                tiles = slice(XC * c, XC * (c + 1))
                sp.wait_ge(x_in[c], 16)
                sp.dma_start(out_tiles[:, tiles, :], x_all[:, tiles, :]).then_inc(out_init, 16)
            with sp.Fori(1, E * HT // RAW) as m:
                for c in range(RAW):
                    sp.wait_ge(w1_T, RAW * m + (c - RAW + 1))
                    load_w1(m * (RAW * P) + c * P, c)
                    sp.wait_ge(w2_ready, RAW * m + (c - RAW + 1))
                    sp.dma_start(w2_raw[:, c, :], w2_rows[ds(m * (RAW * P) + c * P, P), :]).then_inc(w2_in[c], 16)

        @block.gpsimd
        def _(pool):
            chain = [0]

            def link(ins):
                chain[0] += 1
                ins.then_inc(pool_chain, 1)
                pool.wait_ge(pool_chain, chain[0])

            link(pool.memset(ident[:, :], 0.0))
            pool.affine_select(out=ident[:, :], in_=ident[:, :], compare_op=ALU.not_equal, fill=1.0, base=0,
                               pattern=[[-1, P]], channel_multiplier=1).then_inc(consts_ready, 1)
            pool.iota(part_i[:, :], pattern=[[0, 1]], base=0, channel_multiplier=1)
            pool.iota(j1[:, :], pattern=[[1, TJ]], base=1, channel_multiplier=0, allow_small_or_imprecise_dtypes=True)
            pool.iota(first_i[:, :], pattern=[[-1, E]], base=E, channel_multiplier=0)
            pool.iota(expert_i[:, :], pattern=[[1, E], [0, BLOCKS // E]], base=0, channel_multiplier=0)
            pool.iota(base_i[:, :], pattern=[[CAP, E]], base=0, channel_multiplier=0).then_inc(consts_ready, 1)
            pool.iota(value[:, :, :], pattern=[[1, P], [0, TJ]], base=0, channel_multiplier=0,
                      allow_small_or_imprecise_dtypes=True)
            link(pool.memset(ones[:, :], 1.0))
            link(pool.memset(carry[:, :, :], 1.0))
            pool.memset(carry[:, :, 0:1], 0.0)
            pool.affine_select(out=before[:, :], in_=ones[:, :], compare_op=ALU.is_gt, fill=0.0, base=0,
                               pattern=[[1, P]], channel_multiplier=-1).then_inc(consts_ready, 1)

            pool.wait_ge(gates_ready, 1)
            pool.dma_start(gates_dram.rearrange("(p j e) a -> p j (e a)", j=TJ, e=E), gm[:, :, :]).then_inc(gates_stored, 16)
            pool.wait_ge(slots_ready, 1)

            def take_rows(s, par):
                pool.tensor_copy(gather_now[:, par, :], gather_row[:, ds(SB * s, SB)]).then_inc(now_ready, 1)
                pool.tensor_copy(scatter_now[:, par, :], scatter_row[:, ds(SB * s, SB)]).then_inc(now_ready, 1)
                pool.tensor_copy(gate_at_now[:, par, :], gate_row[:, ds(SB * s, SB)]).then_inc(now_ready, 1)
                pool.wait_ge(now_ready, 3 * (s + 1))
                pool.nop(nofuse=True)

            def gather_x(s, par, u, first=False):
                if not first:
                    pool.wait_ge(x_T, 4 * s + 2 * u)
                    pool.nop(nofuse=True)
                for bb in range(2):
                    b = 2 * u + bb
                    pool.indirect_dma_start(
                        x_blk[:, bb, :], None, x_rows,
                        bass.IndirectOffsetOnAxis(ap=gather_now[:, par, b:b + 1], axis=0)).then_inc(blk_in[bb], 16)

            def gather_rows(par):
                for b in range(SB):
                    pool.indirect_dma_start(
                        rows[:, b, :], None, out_rows,
                        bass.IndirectOffsetOnAxis(ap=gather_now[:, par, b:b + 1], axis=0)).then_inc(rows_in, 16)
                    pool.indirect_dma_start(
                        gate_now[:, b:b + 1], None, gates_dram,
                        bass.IndirectOffsetOnAxis(ap=gate_at_now[:, par, b:b + 1], axis=0)).then_inc(rows_in, 16)

            take_rows(0, 0)
            for b in range(SB):
                pool.indirect_dma_start(
                    rows[:, b, :], None, x_rows,
                    bass.IndirectOffsetOnAxis(ap=gather_now[:, 0, b:b + 1], axis=0)).then_inc(x0_in[b], 16)
            take_rows(1, 1)
            gather_x(1, 1, 0, first=True)
            pool.dma_start(b2_bc[:, :], b2_rows[0:1, :].partition_broadcast(P)).then_inc(b2_in, 16)
            pool.wait_ge(gates_stored, 16)
            pool.wait_ge(out_init, 16 * CHUNKS)
            pool.wait_ge(x_T, SB)
            gather_rows(0)
            gather_x(1, 1, 1)

            def expert(e, last):
                for half in range(SLABS):
                    s = e * SLABS + half
                    end = last and half == SLABS - 1
                    for b in range(SB):
                        pool.wait_ge(sums_ready, SB * (s + 1) + b + 1)
                        pool.nop(nofuse=True)
                        pool.indirect_dma_start(
                            out_rows, bass.IndirectOffsetOnAxis(ap=scatter_now[:, half, b:b + 1], axis=0),
                            rows[:, b, :], None, bounds_check=TOKENS - 1, oob_is_err=False).then_inc(rows_out, 16)
                    pool.wait_ge(rows_out, (s + 1) * (16 * SB))
                    pool.nop(nofuse=True)
                    if not (last and half >= SLABS - 2):
                        take_rows(s + 2, half)
                        gather_x(s + 2, half, 0)
                    if not end:
                        if half == SLABS - 1:
                            pool.dma_start(b2_bc[:, :], b2_rows[ds(e + 1, 1), :].partition_broadcast(P)
                                           ).then_inc(b2_in, 16)
                        gather_rows((half + 1) % 2)
                    if not (last and half >= SLABS - 2):
                        gather_x(s + 2, half, 1)

            experts(pool, expert)

        @block.scalar
        def _(act):
            act.wait_ge(squares_ready, 1)
            act.activation(nrm[:, 2:4], nrm[:, 0:2], ACT.Sqrt).then_inc(norms_ready, 1)
            def keep_logits(g):
                act.wait_ge(xT_used, Q * (g + 1))
                if g >= 2:
                    act.wait_ge(logits_T, g - 1)
                act.activation(logitsT[:, g % 2, :], hp[0:2 * E, g % 2, :], ACT.Copy).then_inc(logitsT_kept, 1)

            for u in range(UNITS):
                act.wait_ge(xT_ps, u + 1)
                if u >= 2:
                    act.wait_ge(xT_used, u - 1)
                act.activation(xT_hi[:, u % 2, :], eo[:, u % Q, :], ACT.Copy).then_inc(xT_hi_ready, 1)
                if u % Q == Q - 1 and u >= Q:
                    keep_logits(u // Q - 1)
            keep_logits(CHUNKS - 1)
            act.wait_ge(shifted, 1)
            act.activation(ex[:, :, :], dl[:, :, :], ACT.Exp).then_inc(exps_ready, 1)
            act.wait_ge(slots_ready, 1)
            act.wait_ge(out_init, 16 * CHUNKS)

            def make_tile(e, hh, n, c):
                act.wait_ge(w1_T, n + 1)
                act.activation(w1T_hi[:, hh, :, :], w1_turned[:, c, :, :], ACT.Copy).then_inc(w1_hi_ready, 1)
                act.wait_ge(w2_in[c], 16 * e * (HT // RAW) + 16 * (hh // RAW + 1))
                act.activation(w2_hi[:, hh, :], w2_raw[:, c, :], ACT.Copy).then_inc(w2_hi_ready, 1)

            def hidden(g, hh, first=0):
                c = hh % 2
                act.wait_ge(fc1_done, g + 1)
                if first == 0:
                    act.wait_ge(fc2_done, g * SB)
                act.activation(h_hi[:, c, :], hp[:, c, :], ACT.Relu, bias=b1_now[:, hh:hh + 1]).then_inc(h_hi_ready, 1)
                if first < 2:
                    act.wait_ge(h_ready, g + 1)
                act.activation(h_full[:, :], hp[:, c, :], ACT.Relu, bias=b1_now[:, hh:hh + 1]).then_inc(h_full_ready, 1)

            def split_y(s, par, u):
                act.wait_ge(rotated, 8 * s + 4 * u + 8)
                act.activation(yT_hi[:, par, :, u * HALF:(u + 1) * HALF], y_half[:, :, :], ACT.Copy
                               ).then_inc(y_hi_ready, 1)

            for n in range(AHEAD):
                make_tile(0, n, n, n)
            for i in range(Q + 1):
                if i < Q:
                    act.wait_ge(x_T, SB)
                    if i >= 2:
                        act.wait_ge(y_ready, i - 1)
                    act.activation(y_sum[:, i % 2, :], eo[:, 0, :], ACT.Copy, scale=rot[:, i, 0:1]).then_inc(y0_begun, 1)
                if i >= 1:
                    act.wait_ge(rotated, 3 * i)
                    act.activation(yT_hi[:, 0, i - 1, :], y_sum[:, (i - 1) % 2, :], ACT.Copy).then_inc(y_hi_ready, 1)
            act.wait_ge(b1_kept, 1)
            act.activation(b1_now[:, :], b1T[:, 0:HT], ACT.Copy).then_inc(b1_taken, 1)
            act.wait_ge(b1_taken, 1)
            hidden(0, 0, first=2)

            def expert(e, last):
                for half in range(SLABS):
                    for hh in range(HT):
                        end = last and half == SLABS - 1
                        g = e * STEPS + half * HT + hh
                        if half == 0 and hh + AHEAD < HT:
                            make_tile(e, hh + AHEAD, e * HT + hh + AHEAD, hh % RAW)
                        if half == SLABS - 1 and hh + AHEAD >= HT and not last:
                            make_tile(e + 1, hh + AHEAD - HT, e * HT + hh + AHEAD, hh % RAW)
                        if not (end and hh == HT - 1):
                            if hh == HT - 1 and half == SLABS - 1:
                                act.wait_ge(b1_found, e + 1)
                                act.wait_ge(h_full_ready, g + 1)
                                act.activation(b1_now[:, :], b1_next[:, :], ACT.Copy).then_inc(b1_taken, 1)
                                act.wait_ge(b1_taken, e + 2)
                            hidden(g + 1, (hh + 1) % HT)
                        if half == SLABS - 1 and hh == HT // 2 and not last:
                            act.activation(b1_next[:, :], b1T[:, ds((e + 1) * HT, HT)], ACT.Copy).then_inc(b1_found, 1)
                        if hh in FINISH_AT and not end:
                            split_y(e * SLABS + half + 1, (half + 1) % 2, FINISH_AT.index(hh))

            experts(act, expert)

        @block.vector
        def _(dve):
            chain = [0]

            def link(ins):
                chain[0] += 1
                ins.then_inc(dve_chain, 1)
                dve.wait_ge(dve_chain, chain[0])

            dve.wait_ge(small_T, 1)
            link(dve.tensor_copy(qq[:, :], small_ps))
            link(dve.tensor_tensor(sq[:, :, :].rearrange("p a q -> p (a q)"), qq[:, 0:2 * Q], qq[:, 0:2 * Q], ALU.mult))
            link(dve.tensor_reduce(nrm[:, 0:2], sq[:, :, :], X, ALU.add))
            dve.tensor_scalar(nrm[:, 0:2], nrm[:, 0:2], 1e-8, None, ALU.add).then_inc(squares_ready, 1)
            dve.wait_ge(norms_ready, 1)
            link(dve.reciprocal(nrm[:, 0:2], nrm[:, 2:4]))
            for a in range(2):
                lastop = dve.tensor_scalar(qn[:, a, :], qq[:, a * Q:(a + 1) * Q], nrm[:, a:a + 1], None, ALU.mult)
            link(lastop)
            link(dve.tensor_scalar(qn[:, 1, 1:Q], qn[:, 1, 1:Q], -1.0, None, ALU.mult))
            link(dve.tensor_scalar(neg[:, :, :], qn[:, :, :], -1.0, None, ALU.mult))
            LEFT = [[(0, 1), (1, -1), (2, -1), (3, -1)], [(1, 1), (0, 1), (3, -1), (2, 1)],
                    [(2, 1), (3, 1), (0, 1), (1, -1)], [(3, 1), (2, -1), (1, 1), (0, 1)]]
            RIGHT = [[(0, 1), (1, -1), (2, -1), (3, -1)], [(1, 1), (0, 1), (3, 1), (2, -1)],
                     [(2, 1), (3, -1), (0, 1), (1, 1)], [(3, 1), (2, 1), (1, -1), (0, 1)]]
            for a, (table, dst) in enumerate(((LEFT, Lm), (RIGHT, Rm))):
                for i in range(Q):
                    for j in range(Q):
                        k, sign = table[i][j]
                        lastop = dve.tensor_copy(dst[:, i, j:j + 1], (qn if sign > 0 else neg)[:, a, k:k + 1])
            link(lastop)
            link(dve.tensor_scalar(Rm[:, :, :], Rm[:, :, :], qq[:, 2 * Q:2 * Q + 1], None, ALU.mult))
            for m in range(Q):
                dst = rot if m == 0 else rt
                link(dve.tensor_tensor(dst[:, :, :], Lm[:, :, m:m + 1].to_broadcast([P, Q, Q]),
                                       Rm[:, m:m + 1, :].to_broadcast([P, Q, Q]), ALU.mult))
                if m:
                    link(dve.tensor_tensor(rot[:, :, :], rot[:, :, :], rt[:, :, :], ALU.add))
            link(dve.tensor_copy(gwT[:, :, :].rearrange("p q e -> p (q e)"), gw_ps))
            for i in range(Q):
                dst = grot if i == 0 else gt
                ins = dve.tensor_tensor(dst[:, :, :], gwT[:, i:i + 1, :].to_broadcast([P, Q, E]),
                                        rot[:, i, :].unsqueeze(2).to_broadcast([P, Q, E]), ALU.mult)
                link(ins)
                if i:
                    link(dve.tensor_tensor(grot[:, :, :], grot[:, :, :], gt[:, :, :], ALU.add))
            link(dve.tensor_copy(grot_hl[:, :, 0:E], grot[:, :, :]))
            dve.tensor_tensor(grot_hl[:, :, E:2 * E], grot[:, :, :], grot_hl[:, :, 0:E].bitcast(F32), ALU.subtract
                              ).then_inc(grot_ready, 1)
            dve.tensor_copy(b1T[:, :], b1_ps).then_inc(b1_kept, 1)
            dve.wait_ge(consts_ready, 2)
            dve.tensor_copy(part_f[:, :], part_i[:, :]).then_inc(h_ready, 1)
            dve.tensor_copy(first_f[:, :], first_i[:, :])
            dve.tensor_copy(expert_f[:, :], expert_i[:, :])
            link(dve.tensor_copy(base_f[:, :], base_i[:, :]))

            for u in range(UNITS):
                dve.wait_ge(xT_hi_ready, u + 1)
                dve.tensor_tensor(xT_lo[:, u % 2, :], eo[:, u % Q, :], xT_hi[:, u % 2, :].bitcast(F32), ALU.subtract
                                  ).then_inc(xT_ready, 1)

            def per_e(ap):
                return ap.unsqueeze(2).to_broadcast([P, TJ, E])

            mx, sm, v1, v2, w1m, w2m, gs, g1, g2, e1 = (st[:, k, :] for k in range(10))
            dve.wait_ge(logits_T, CHUNKS)
            link(dve.tensor_copy(lg_low[:, :, :], logits_hl[:, :, 1, :]))
            link(dve.tensor_tensor(lg[:, :, :], logits_hl[:, :, 0, :], lg_low[:, :, :], ALU.add))
            link(dve.reduce_max(mx, lg[:, :, :], X))
            dve.tensor_tensor(dl[:, :, :], lg[:, :, :], per_e(mx), ALU.subtract).then_inc(shifted, 1)
            dve.wait_ge(exps_ready, 1)
            link(dve.reduce_sum(sm, ex[:, :, :], X))
            link(dve.reciprocal(sm, sm))
            link(dve.tensor_tensor(score[:, :, :], ex[:, :, :], per_e(sm), ALU.mult))
            first_bc = first_f[:, :].unsqueeze(1).to_broadcast([P, TJ, E])
            for k, (v, w) in enumerate(((v1, w1m), (v2, w2m))):
                hot_k = hot[:, k, :, :].rearrange("p e j -> p j e")
                link(dve.reduce_max(v, score[:, :, :], X))
                link(dve.tensor_tensor(wt[:, :, :], score[:, :, :], per_e(v), ALU.is_equal))
                link(dve.tensor_tensor(wt[:, :, :], wt[:, :, :], first_bc, ALU.mult))
                link(dve.reduce_max(w, wt[:, :, :], X))
                link(dve.tensor_tensor(hot_k, wt[:, :, :], per_e(w), ALU.is_equal))
                if k == 0:
                    link(dve.scalar_tensor_tensor(score[:, :, :], hot_k, -2.0, score[:, :, :], ALU.mult, ALU.add))
            dve.wait_ge(consts_ready, 3)
            cnt2 = cnt[:, :, :].rearrange("p k j -> p (k j)")
            link(dve.tensor_tensor_scan(cnt2, carry[:, :, :].rearrange("p k j -> p (k j)"),
                                        hot[:, :, :, :].rearrange("p k e j -> p (k e j)"), 0.0, ALU.mult, ALU.add))
            dve.tensor_copy(tot[:, :], cnt[:, :, TJ - 1]).then_inc(counts_ready, 1)
            dve.wait_ge(ahead_ready, 1)
            ke = [P, TOPK * E, TJ]
            hot3 = hot[:, :, :, :].rearrange("p k e j -> p (k e) j")
            link(dve.tensor_tensor(cnt[:, :, :], cnt[:, :, :], ahead_ps.unsqueeze(2).to_broadcast(ke), ALU.add))
            link(dve.scalar_tensor_tensor(loc[:, :, :], cnt[:, :, :], float(CAP), hot3, ALU.is_le, ALU.mult))
            for k in range(TOPK):
                part = cnt[:, k * E:(k + 1) * E, :]
                ins = dve.tensor_tensor(part, part, base_f[:, :].unsqueeze(2).to_broadcast([P, E, TJ]), ALU.add)
            link(ins)
            link(dve.tensor_tensor(loc[:, :, :], loc[:, :, :], cnt[:, :, :], ALU.mult))
            link(dve.reduce_sum(slot1[:, :, :], loc[:, :, :].rearrange("p (k e) j -> p k j e", k=TOPK), X))
            link(dve.tensor_scalar(slot_i[:, :], slot1[:, :, :].rearrange("p k j -> p (k j)"), -1.0, None, ALU.add))
            dve.tensor_scalar(q_i[:, :], slot_i[:, :], 7, None, ALU.arith_shift_right)
            link(dve.tensor_scalar(b_i[:, :], slot_i[:, :], P - 1, None, ALU.bitwise_and))
            dve.tensor_copy(q_f[:, :, :].rearrange("p k j -> p (k j)"), q_i[:, :]).then_inc(sums_ready, SB)
            link(dve.tensor_copy(b_f[:, :, :].rearrange("p k j -> p (k j)"), b_i[:, :]))
            for k in range(TOPK):
                dve.tensor_tensor(hot_b[:, k, :, :], value[:, :, :], b_f[:, k:k + 1, :].to_broadcast([P, P, TJ]),
                                  ALU.is_equal)
                link(dve.tensor_tensor(hot_q[:, k, 0, :, :], value[:, 0:BLOCKS, :],
                                       q_f[:, k:k + 1, :].to_broadcast([P, BLOCKS, TJ]), ALU.is_equal))
                link(dve.tensor_scalar(hot_q[:, k, 1, :, :], hot_q[:, k, 0, :, :], part_f[:, :], None, ALU.mult))
                dve.tensor_tensor(hot_q[:, k, 0, :, :], hot_q[:, k, 0, :, :],
                                  j1[:, :].unsqueeze(1).to_broadcast([P, BLOCKS, TJ]), ALU.mult).then_inc(hots_ready, 1)
            link(dve.tensor_tensor(gs, v1, v2, ALU.add))
            link(dve.reciprocal(gs, gs))
            dve.tensor_tensor(g1, v1, gs, ALU.mult)
            link(dve.tensor_tensor(g2, v2, gs, ALU.mult))
            dve.tensor_tensor(gm[:, :, :], hot[:, 0, :, :].rearrange("p e j -> p j e"), per_e(g1), ALU.mult)
            link(dve.tensor_tensor(wt[:, :, :], hot[:, 1, :, :].rearrange("p e j -> p j e"), per_e(g2), ALU.mult))
            dve.tensor_tensor(gm[:, :, :], gm[:, :, :], wt[:, :, :], ALU.add).then_inc(gates_ready, 1)
            dve.wait_ge(hots_used, TOPK)
            link(dve.tensor_copy(j_part[:, :], token_ps[:, 0, :]))
            link(dve.scalar_tensor_tensor(token1[:, :], token_ps[:, 1, :], float(TJ), j_part[:, :], ALU.mult, ALU.add))
            dve.tensor_scalar(gather_row[:, :], token1[:, :], -1.0, 0.0, ALU.add, ALU.max)
            dve.tensor_scalar(gate_f[:, :], token1[:, :], -1.0, 0.0, ALU.add, ALU.max)
            link(dve.tensor_scalar(skip[:, :], token1[:, :], 0.0, float(SKIP), ALU.is_equal, ALU.mult))
            dve.scalar_tensor_tensor(gate_row[:, :], gate_f[:, :], float(E), expert_f[:, :], ALU.mult, ALU.add)
            dve.scalar_tensor_tensor(scatter_row[:, :], token1[:, :], -1.0, skip[:, :], ALU.add, ALU.add
                                     ).then_inc(slots_ready, 1)

            def turn_tile(e, hh, n, c):
                dve.wait_ge(w1_in[c], 16 * W1_DMAS * (e * (HT // RAW) + (hh // RAW + 1)))
                dve.wait_ge(w1_ready, n - 1)
                dve.transpose(w1_turned[:, c, :, :].rearrange("p q n -> p (q n)"), w1_raw[:, c, :]).then_inc(w1_T, 1)

            def make_tile(hh, n, c):
                dve.wait_ge(w1_hi_ready, n + 1)
                dve.tensor_tensor(w1T_lo[:, hh, :, :], w1_turned[:, c, :, :], w1T_hi[:, hh, :, :].bitcast(F32), ALU.subtract
                                  ).then_inc(w1_ready, 1)
                dve.wait_ge(w2_hi_ready, n + 1)
                dve.tensor_tensor(w2_lo[:, hh, :], w2_raw[:, c, :], w2_hi[:, hh, :].bitcast(F32), ALU.subtract
                                  ).then_inc(w2_ready, 1)

            def hidden_low(g, c):
                dve.wait_ge(h_full_ready, g + 1)
                dve.tensor_tensor(h_lo[:, c, :], h_full[:, :], h_hi[:, c, :].bitcast(F32), ALU.subtract
                                  ).then_inc(h_ready, 1)

            def rotate(s, k, jj):
                j = 2 * (k % 2) + jj
                if jj == 0:
                    dve.wait_ge(x_T, 4 * s + k + 1)
                for i in range(Q):
                    if j == 0:
                        if i == 0:
                            dve.wait_ge(y_ready, 2 * s + k // 2 + 2)
                        ins = dve.tensor_scalar(y_half[:, i, :], xp[:, jj, :], rot[:, i, j:j + 1], None, ALU.mult)
                    else:
                        if i == 0:
                            dve.wait_ge(rotated, 8 * s + 2 * k + jj + 4)
                        ins = dve.scalar_tensor_tensor(y_half[:, i, :], xp[:, jj, :], rot[:, i, j:j + 1],
                                                       y_half[:, i, :], ALU.mult, ALU.add)
                ins.then_inc(rotated, 1)

            def split_y(s, par, u):
                dve.wait_ge(y_hi_ready, 2 * s + u + 3)
                dst = slice(u * HALF, (u + 1) * HALF)
                dve.tensor_tensor(yT_lo[:, par, :, dst], y_half[:, :, :], yT_hi[:, par, :, dst].bitcast(F32),
                                  ALU.subtract).then_inc(y_ready, 1)

            for n in range(AHEAD):
                dve.wait_ge(w1_in[n], 16 * W1_DMAS)
                dve.transpose(w1_turned[:, n, :, :].rearrange("p q n -> p (q n)"), w1_raw[:, n, :]).then_inc(w1_T, 1)
                make_tile(n, n, n)
            def first_low(i):
                dve.wait_ge(y_hi_ready, i + 1)
                dve.tensor_tensor(yT_lo[:, 0, i, :], y_sum[:, i % 2, :], yT_hi[:, 0, i, :].bitcast(F32), ALU.subtract
                                  ).then_inc(y_ready, 1)

            for i in range(Q):
                dve.wait_ge(y0_begun, i + 1)
                for j in range(1, Q):
                    if j > 1:
                        dve.wait_ge(rotated, 3 * i + j - 1)
                    dve.scalar_tensor_tensor(y_sum[:, i % 2, :], eo[:, j, :], rot[:, i, j:j + 1], y_sum[:, i % 2, :],
                                             ALU.mult, ALU.add).then_inc(rotated, 1)
                if i:
                    first_low(i - 1)
            first_low(Q - 1)
            hidden_low(0, 0)

            def expert(e, last):
                for half in range(SLABS):
                    s = e * SLABS + half
                    end = last and half == SLABS - 1
                    for hh in range(HT):
                        g = e * STEPS + half * HT + hh
                        tile = e * HT + hh + AHEAD
                        if half == 0 and hh + AHEAD < HT:
                            turn_tile(e, hh + AHEAD, tile, hh % RAW)
                            make_tile(hh + AHEAD, tile, hh % RAW)
                        if half == SLABS - 1 and hh + AHEAD >= HT and not last:
                            turn_tile(e + 1, hh + AHEAD - HT, tile, hh % RAW)
                            make_tile(hh + AHEAD - HT, tile, hh % RAW)
                        if not end:
                            for k, at in enumerate(ROT_AT):
                                if hh in (at, at + 1):
                                    rotate(s + 1, k, hh - at)
                            if hh in FINISH_AT:
                                split_y(s + 1, (half + 1) % 2, FINISH_AT.index(hh))
                        if hh in PRE_AT:
                            b = PRE_AT.index(hh)
                            if b == 0:
                                dve.wait_ge(rows_in, (s + 1) * (32 * SB))
                                dve.wait_ge(b2_in, 16 * (e + 1))
                            dve.scalar_tensor_tensor(rows[:, b, :], b2_bc[:, :], gate_now[:, b:b + 1], rows[:, b, :],
                                                     ALU.mult, ALU.add).then_inc(pre_done, 1)
                        if not (end and hh == HT - 1):
                            hidden_low(g + 1, (hh + 1) % 2)
                        if hh == HT - 1:
                            for b in range(SB):
                                dve.wait_ge(fc2_done, (g + 1) * SB + b + 1)
                                dve.wait_ge(pre_done, SB * s + b + 1)
                                dve.scalar_tensor_tensor(rows[:, b, :], eo[:, b, :], gate_now[:, b:b + 1],
                                                         rows[:, b, :], ALU.mult, ALU.add).then_inc(sums_ready, 1)

            experts(dve, expert)

        @block.tensor
        def _(pe):
            pe.wait_ge(consts_ready, 1)
            pe.wait_ge(small_in, 48)
            pe.wait_ge(gw_in, 16)
            pe.transpose(small_ps, small[0:9, :], ident[0:9, 0:9]).then_inc(fc2_done, SB)
            for q in range(Q):
                ins = pe.transpose(gw_ps[:, q * E:(q + 1) * E], gw_nat[:, q * P:(q + 1) * P], ident[0:E, 0:E])
            pe.wait_ge(b1_in, 16)
            pe.transpose(b1_ps, b1_nat[:, :], ident[:, :]).then_inc(small_T, 1)

            def take_logits(u):
                bank = hp[0:2 * E, (u // Q) % 2, :]
                q = u % Q
                pe.wait_ge(xT_ready, u + 1)
                if q == 0 and u >= 2 * Q:
                    pe.wait_ge(logitsT_kept, u // Q - 1)
                pe.matmul(bank, grot_hl[:, q, :], xT_hi[:, u % 2, :], start=(q == 0), stop=False)
                pe.matmul(bank, grot_hl[:, q, :], xT_lo[:, u % 2, :], start=False, stop=(q == Q - 1)).then_inc(xT_used, 1)

            def turn_logits(g):
                pe.wait_ge(logitsT_kept, g + 1)
                for t in range(XC):
                    at = (g * XC + t) * 2 * E
                    ins = pe.transpose(xp_all[:, at:at + 2 * E], logitsT[:, g % 2, t * P:(t + 1) * P],
                                       ident[0:2 * E, 0:2 * E])
                ins.then_inc(logits_T, 1)

            for u in range(UNITS + 2):
                if u < UNITS:
                    if u % Q == 0:
                        pe.wait_ge(x_in[u // Q], 16)
                    for t in range(XC):
                        ins = pe.transpose(eo[:, u % Q, t * P:(t + 1) * P],
                                           x_all[:, (u // Q) * XC + t, (u % Q) * P:(u % Q + 1) * P], ident[:, :])
                    ins.then_inc(xT_ps, 1)
                if u == 2:
                    pe.wait_ge(grot_ready, 1)
                if u >= 2:
                    take_logits(u - 2)
                if u % Q == 1 and u >= 2 * Q:
                    turn_logits(u // Q - 2)
            turn_logits(CHUNKS - 1)

            pe.wait_ge(consts_ready, 3)
            pe.wait_ge(counts_ready, 1)
            pe.matmul(ahead_ps, before[:, :], tot[:, :], start=True, stop=False)
            pe.matmul(ahead_ps[:, E:2 * E], ones[:, :], tot[:, 0:E], start=False, stop=True).then_inc(ahead_ready, 1)

            def transpose_x(s, k):
                if k % 2 == 0:
                    for bb in range(2):
                        pe.wait_ge(blk_in[bb], 32 * s + 16 * (k // 2) - 16)
                pe.wait_ge(rotated, 8 * s + 2 * k + 4)
                for jj in range(2):
                    for bb in range(2):
                        j = 2 * (k % 2) + jj
                        ins = pe.transpose(xp[:, jj, bb * P:(bb + 1) * P], x_blk[:, bb, j * P:(j + 1) * P], ident[:, :])
                ins.then_inc(x_T, 1)

            def fc1(g, tile, hh, par, first=False):
                pe.wait_ge(w1_ready, tile + 1)
                if not first:
                    pe.wait_ge(h_ready, g)
                bank = hp[:, hh % 2, :]
                for q in range(Q):
                    if first:
                        pe.wait_ge(y_ready, q + 1)
                    pe.matmul(bank, w1T_hi[:, hh, q, :], yT_hi[:, par, q, :], start=(q == 0), stop=False)
                    pe.matmul(bank, w1T_hi[:, hh, q, :], yT_lo[:, par, q, :], start=False, stop=False)
                    ins = pe.matmul(bank, w1T_lo[:, hh, q, :], yT_hi[:, par, q, :], start=False, stop=(q == Q - 1))
                ins.then_inc(fc1_done, 1)

            def fc2(e, g, s, hh, c):
                pe.wait_ge(w2_ready, e * HT + hh + 1)
                pe.wait_ge(h_hi_ready, g + 1)
                for b in range(SB):
                    if hh == 0:
                        pe.wait_ge(sums_ready, SB * s + (b + 1))
                    blk = slice(b * P, (b + 1) * P)
                    pe.matmul(eo[:, b, :], h_hi[:, c, blk], w2_hi[:, hh, :], start=(hh == 0), stop=False)
                    pe.matmul(eo[:, b, :], h_hi[:, c, blk], w2_lo[:, hh, :], start=False, stop=False)
                pe.wait_ge(h_ready, g + 2)
                for b in range(SB):
                    blk = slice(b * P, (b + 1) * P)
                    pe.matmul(eo[:, b, :], h_lo[:, c, blk], w2_hi[:, hh, :], start=False, stop=(hh == HT - 1)
                              ).then_inc(fc2_done, 1)

            for k in range(TOPK):
                pe.wait_ge(hots_ready, k + 1)
                for j in range(TJ):
                    ins = pe.matmul(token_ps, hot_b[:, k, :, j], hot_q[:, k, :, :, j],
                                    start=(k == 0 and j == 0), stop=(k == TOPK - 1 and j == TJ - 1))
                ins.then_inc(hots_used, 1)
            for b in range(SB):
                pe.wait_ge(x0_in[b], 16)
                for j in range(Q):
                    ins = pe.transpose(eo[:, j, b * P:(b + 1) * P], rows[:, b, j * P:(j + 1) * P], ident[:, :])
                ins.then_inc(x_T, 1)
            fc1(0, 0, 0, 0, first=True)

            def expert(e, last):
                for half in range(SLABS):
                    s = e * SLABS + half
                    end = last and half == SLABS - 1
                    for hh in range(HT):
                        g = e * STEPS + half * HT + hh
                        if hh in ROT_AT and not end:
                            transpose_x(s + 1, ROT_AT.index(hh))
                        if hh < HT - 1:
                            fc1(g + 1, e * HT + hh + 1, hh + 1, half)
                        elif not end:
                            pe.wait_ge(y_ready, 2 * (s + 3))
                            fc1(g + 1, e * HT + (HT if half == SLABS - 1 else 0), 0, (half + 1) % 2)
                        fc2(e, g, s, hh, hh % 2)

            experts(pe, expert)


_INS = ['x', 'cond_256', 'L0_cond_q_right', 'L0_cond_spectral_gate', 'L0_ffn_gate_w', 'L0_ffn_fc1_w',
        'L0_ffn_fc1_b', 'L0_ffn_fc2_w', 'L0_ffn_fc2_b']


def kernel(**inputs):
    import numpy as _np
    import concourse.bacc as _bacc
    from concourse import mybir as _mybir
    from concourse.bass_utils import run_bass_kernel_spmd as _run

    nc = _bacc.Bacc("TRN2", target_bir_lowering=False, num_devices=1)
    arrays, args = {}, []
    for name in _INS:
        a = _np.ascontiguousarray(inputs[name])
        arrays[f"in_{name}"] = a
        args.append(nc.dram_tensor(f"in_{name}", a.shape, _mybir.dt.from_np(a.dtype), kind="ExternalInput").ap())
    shape = tuple(inputs["x"].shape)
    args.append(nc.dram_tensor("out_0", shape, _mybir.dt.float32, kind="ExternalOutput").ap())
    program(nc, *args)
    r = _run(nc, [arrays], core_ids=[0])
    return r.results[0]["out_0"]
```

```python
from contextlib import ExitStack

import concourse.bass as bass
from concourse import mybir

F32 = mybir.dt.float32
F32R = mybir.dt.float32r
I32 = mybir.dt.int32
BF16 = mybir.dt.bfloat16
ACT = mybir.ActivationFunctionType
ALU = mybir.AluOpType
X = mybir.AxisListType.X
ds = bass.ds

P = 128


def program(nc, x, cond, q_right, spectral, gate_w, fc1_w, fc1_b, fc2_w, fc2_b, out):
    B, S, D = x.shape
    E, H, _ = fc1_w.shape
    TOKENS = B * S
    TOPK = 2
    CAP = TOPK * (TOKENS // E)
    Q = D // P
    TJ = TOKENS // P
    HT = H // P
    SLAB = 512
    SB = SLAB // P
    SLABS = CAP // SLAB
    BLOCKS = E * CAP // P
    STEPS = SLABS * HT
    AHEAD = 2
    RAW = 2
    HALF = SLAB // 2
    STORE_AT = (0, 6)
    CUT_AT = (1, 7)
    CUT_PARTS = ((0, 1, 2), (3, 4, 5), (6, 7))
    TURN_AT = (5, 10)
    ROT_AT = (5, 10)
    HI_AT, LO_AT = (8, 13), (9, 14)
    PRE_AT = (7, 10, 12, 14)
    XC = 4
    CHUNKS = TJ // XC
    XBUF = 4
    LAG = 3
    UNITS = CHUNKS * Q
    JH = TJ // 2
    FIRST = 3 * SLABS
    BLK = 32
    CUT_DMAS = P // BLK
    SKIP = 2 * TOKENS

    x_rows = x.rearrange("b s d -> (b s) d")
    x_tiles = x_rows.rearrange("(p j) d -> p j d", j=TJ)
    out_rows = out.rearrange("b s d -> (b s) d")
    out_tiles = out_rows.rearrange("(p j) d -> p j d", j=TJ)
    w1_rows = fc1_w.rearrange("e h d -> (e h) d")
    w2_rows = fc2_w.rearrange("e h d -> (e h) d")
    b2_rows = fc2_b.rearrange("e a d -> (e a) d")
    slots_dram = nc.dram_tensor("slots_dram", [2, 2, P, D], F32, kind="Internal").ap()
    gates_dram = nc.dram_tensor("gates_dram", [TOKENS * E, 1], F32, kind="Internal").ap()

    ctx = ExitStack()
    with ctx:
        def sb(name, shape, dt=F32, where=ctx):
            return where.enter_context(nc.sbuf_tensor(name, shape, dt))

        def sem(name):
            return ctx.enter_context(nc.semaphore(name))

        ident = sb("ident", [P, P])
        rot = sb("rot", [P, Q, Q])
        b1T = sb("b1T", [P, E * HT])
        gather_row = sb("gather_row", [P, BLOCKS], I32)
        scatter_row = sb("scatter_row", [P, BLOCKS], I32)
        gate_row = sb("gate_row", [P, BLOCKS], I32)
        w1T_hi = sb("w1T_hi", [P, HT, Q, P], F32R)
        gm = sb("gm", [P, TJ, E])
        w1_raw = sb("w1_raw", [P, RAW, D])
        w2_raw = sb("w2_raw", [P, RAW, D])
        w1_turned = sb("w1_turned", [P, 2, Q, P])

        early = ExitStack()
        x_all = sb("x_all", [P, TJ, D], where=early)
        value = sb("value", [P, P, TJ], BF16, where=early)
        hot_b = sb("hot_b", [P, TOPK, P, TJ], BF16, where=early)
        transposing = ExitStack()
        xT_hi = sb("xT_hi", [P, XBUF, XC * P], F32R, where=transposing)
        xT_lo = sb("xT_lo", [P, XBUF, XC * P], F32R, where=transposing)
        logitsT = sb("logitsT", [2 * E, 2, XC * P], where=transposing)
        transposing.close()
        hot_t = sb("hot_t", [P, 2, BLOCKS, JH], BF16, where=early)
        hot_q = sb("hot_q", [P, TOPK, 2, BLOCKS, TJ], BF16, where=early)
        small = sb("small", [16, P], where=early)
        gw_nat = sb("gw_nat", [E, D], where=early)
        b1_nat = sb("b1_nat", [E * HT, P], where=early)
        qq = sb("qq", [P, 9], where=early)
        sq = sb("sq", [P, 2, Q], where=early)
        nrm = sb("nrm", [P, 4], where=early)
        qn = sb("qn", [P, 2, Q], where=early)
        sign = sb("sign", [P, 2, Q, Q], where=early)
        spread = sb("spread", [P, 2, Q, Q], where=early)
        factor = sb("factor", [P, 2, Q, Q], where=early)
        rot_terms = sb("rot_terms", [P, Q, Q, Q], where=early)
        gwT = sb("gwT", [P, Q, E], where=early)
        grot = sb("grot", [P, Q, E], where=early)
        grot_terms = sb("grot_terms", [P, Q, E, Q], where=early)
        grot_hl = sb("grot_hl", [P, Q, 2 * E], F32R, where=early)
        lg_low = sb("lg_low", [P, TJ, E], where=early)
        lg = sb("lg", [P, TJ, E], where=early)
        j1 = sb("j1", [P, TJ], BF16, where=early)
        part_i = sb("part_i", [P, 1], I32, where=early)
        part_f = sb("part_f", [P, 1], where=early)
        first_i = sb("first_i", [P, E], I32, where=early)
        first_f = sb("first_f", [P, E], where=early)
        base_i = sb("base_i", [P, E], I32, where=early)
        base_f = sb("base_f", [P, E], where=early)
        ones = sb("ones", [P, P], where=early)
        before = sb("before", [P, P], where=early)
        carry = sb("carry", [P, TOPK * E, TJ], where=early)
        dl = sb("dl", [P, TJ, E], where=early)
        ex = sb("ex", [P, TJ, E], where=early)
        score = sb("score", [P, TJ, E], where=early)
        wt = sb("wt", [P, TJ, E], where=early)
        st = sb("st", [P, 9, TJ], where=early)
        hot = sb("hot", [P, TOPK, E, TJ], where=early)
        cnt = sb("cnt", [P, TOPK * E, TJ], where=early)
        loc = sb("loc", [P, TOPK * E, TJ], where=early)
        tot = sb("tot", [P, TOPK * E], where=early)
        ahead = sb("ahead", [P, TOPK * E], where=early)
        base_kj = sb("base_kj", [P, TOPK, TJ], where=early)
        place = sb("place", [P, TOPK, TJ], where=early)
        slot1 = sb("slot1", [P, TOPK, TJ], where=early)
        slot_i = sb("slot_i", [P, TOPK * TJ], I32, where=early)
        q_i = sb("q_i", [P, TOPK * TJ], I32, where=early)
        b_i = sb("b_i", [P, TOPK * TJ], I32, where=early)
        q_f = sb("q_f", [P, TOPK, TJ], BF16, where=early)
        b_f = sb("b_f", [P, TOPK, TJ], BF16, where=early)
        token1 = sb("token1", [P, BLOCKS], where=early)
        j_part = sb("j_part", [P, BLOCKS], where=early)
        skip = sb("skip", [P, BLOCKS], where=early)
        gate_f = sb("gate_f", [P, BLOCKS], where=early)
        expert_i = sb("expert_i", [P, BLOCKS], I32, where=early)
        expert_f = sb("expert_f", [P, BLOCKS], where=early)
        early.close()

        w2_hi = sb("w2_hi", [P, HT, D], F32R)
        w2_lo = sb("w2_lo", [P, HT, D], F32R)
        w1T_lo = sb("w1T_lo", [P, HT, Q, P], F32R)
        yT_hi = sb("yT_hi", [P, 2, Q, SLAB], F32R)
        yT_lo = sb("yT_lo", [P, 2, Q, SLAB], F32R)
        h_hi = sb("h_hi", [P, 2, SLAB], F32R)
        h_lo = sb("h_lo", [P, 2, SLAB], F32R)
        h_full = sb("h_full", [P, SLAB])
        x_blk = sb("x_blk", [P, 2, D])
        x_turned = sb("x_turned", [P, 2, Q, P])
        y_half = sb("y_half", [P, Q, HALF])
        y_half2 = x_turned[:, :, :, :].rearrange("p b q n -> p (b q n)").rearrange("p (q n) -> p q n", q=Q)
        rows = sb("rows", [P, SB, D])
        b2_bc = sb("b2_bc", [P, D])
        gate_now = sb("gate_now", [P, SB])
        gather_now = sb("gather_now", [P, 2, SB], I32)
        scatter_now = sb("scatter_now", [P, 2, SB], I32)
        gate_at_now = sb("gate_at_now", [P, 2, SB], I32)
        b1_next = sb("b1_next", [P, HT])
        b1_now = sb("b1_now", [P, HT])

        eo = ctx.enter_context(nc.psum_tensor("eo", [P, SB, D], F32))
        hp = ctx.enter_context(nc.psum_tensor("hp", [P, 2, SLAB], F32))
        params_ps = ctx.enter_context(nc.psum_tensor("params_ps", [P, D], F32))
        logits_bank = ctx.enter_context(nc.psum_tensor("logits_bank", [P, D], F32))
        logits_hl = logits_bank[:, :].rearrange("p (j a e) -> p j a e", a=2, e=E)
        ahead_ps = hp[:, 0, 0:TOPK * E]
        token_ps = hp[:, 0, 0:2 * BLOCKS].rearrange("p (a q) -> p a q", a=2)
        small_ps = params_ps[:, 0:2 * Q + 1]
        gw_ps = params_ps[:, 16:16 + Q * E]
        b1_ps = params_ps[:, P:P + E * HT]
        eo_half = eo[:, :, :].rearrange("p a (b n) -> p (a b) n", b=2)

        small_in, gw_in, b1_in = sem("small_in"), sem("gw_in"), sem("b1_in")
        x_in0 = [sem(f"x_in0_{q}") for q in range(Q)]
        x_in = [x_in0] + [[sem(f"x_in{c}")] for c in range(1, CHUNKS)]
        x0_in = [sem(f"x0_in{b}") for b in range(SB)]
        out_init = sem("out_init")
        w1_in = [sem(f"w1_in{c}") for c in range(RAW)]
        w2_in = [sem(f"w2_in{c}") for c in range(RAW)]
        consts_ready, pool_chain = sem("consts_ready"), sem("pool_chain")
        gather_taken, scatter_taken = sem("gather_taken"), sem("scatter_taken")
        small_T, b1_T, b1_kept = sem("small_T"), sem("b1_T"), sem("b1_kept")
        squares_ready, norms_ready, grot_ready = sem("squares_ready"), sem("norms_ready"), sem("grot_ready")
        xT_ps, xT_hi_ready, xT_ready, xT_used = sem("xT_ps"), sem("xT_hi_ready"), sem("xT_ready"), sem("xT_used")
        logitsT_kept, logits_T = sem("logitsT_kept"), sem("logits_T")
        y0_begun, part_ready = sem("y0_begun"), sem("part_ready")
        shifted, exps_ready, counts_ready, ahead_ready = (
            sem("shifted"), sem("exps_ready"), sem("counts_ready"), sem("ahead_ready"))
        gates_ready, gates_stored = sem("gates_ready"), sem("gates_stored")
        hot_t_ready, hots_p_ready = sem("hot_t_ready"), sem("hots_p_ready")
        hots_ready, hots_used, slots_ready = sem("hots_ready"), sem("hots_used"), sem("slots_ready")
        tables_ready, signs_ready = sem("tables_ready"), sem("signs_ready")
        dve_chain = sem("dve_chain")
        w1_T, w1_hi_ready, w1_ready = sem("w1_T"), sem("w1_hi_ready"), sem("w1_ready")
        w2_hi_ready, w2_ready = sem("w2_hi_ready"), sem("w2_ready")
        blk_in = [sem(f"blk_in{c}") for c in range(2)]
        cut_out, cut_in, cut_T = sem("cut_out"), sem("cut_in"), sem("cut_T")
        x_T, rotated, y_hi_ready, y_ready = sem("x_T"), sem("rotated"), sem("y_hi_ready"), sem("y_ready")
        fc1_done, fc2_done = sem("fc1_done"), sem("fc2_done")
        h_hi_ready, h_full_ready, h_ready = sem("h_hi_ready"), sem("h_full_ready"), sem("h_ready")
        rows_in, b2_in, rows_out = sem("rows_in"), sem("b2_in"), sem("rows_out")
        pre_done, sums_ready, b1_taken, b1_found = (
            sem("pre_done"), sem("sums_ready"), sem("b1_taken"), sem("b1_found"))

        def experts(eng, body):
            with eng.Fori(0, E - 1) as e:
                body(e, False)
            body(E - 1, True)

        def load_cut(eng, to, rows_128, arrived, parts=range(P // BLK)):
            cut = rows_128.rearrange("(hq r) (k dq c) -> dq r k hq c", r=BLK, k=Q, c=BLK)
            for dq in parts:
                part = to[dq * BLK:(dq + 1) * BLK, :].rearrange("r (k hq c) -> r k hq c", k=Q, c=BLK)
                eng.dma_start(part, cut[dq]).then_inc(arrived, 16)

        block = ctx.enter_context(nc.Block())

        @block.sync
        def _(sp):
            sp.dma_start(small[0:Q, :], cond).then_inc(small_in, 16)
            sp.dma_start(small[Q:2 * Q, :], q_right).then_inc(small_in, 16)
            sp.dma_start(small[2 * Q:2 * Q + 1, :], spectral.rearrange("a b c d -> (a b c) d")).then_inc(small_in, 16)
            sp.dma_start(gw_nat[:, :], gate_w).then_inc(gw_in, 16)
            for q in range(Q):
                sp.dma_start(x_all[:, 0:XC, q * P:(q + 1) * P], x_tiles[:, 0:XC, q * P:(q + 1) * P]).then_inc(x_in0[q], 16)
            sp.dma_start(b1_nat[:, :], fc1_b.rearrange("e a (t p) -> (e a t) p", p=P)).then_inc(b1_in, 16)
            for c in range(1, CHUNKS):
                tiles = slice(XC * c, XC * (c + 1))
                sp.dma_start(x_all[:, tiles, :], x_tiles[:, tiles, :]).then_inc(x_in[c][0], 16)

            def load_w1(row, c):
                load_cut(sp, w1_raw[:, c, :], w1_rows[ds(row, P), :], w1_in[c])

            for n in range(RAW):
                load_w1(n * P, n)
                sp.dma_start(w2_raw[:, n, :], w2_rows[n * P:(n + 1) * P, :]).then_inc(w2_in[n], 16)
            for c in range(CHUNKS):
                tiles = slice(XC * c, XC * (c + 1))
                for arrived in x_in[c]:
                    sp.wait_ge(arrived, 16)
                sp.dma_start(out_tiles[:, tiles, :], x_all[:, tiles, :]).then_inc(out_init, 16)
            with sp.Fori(1, E * HT // RAW) as m:
                for c in range(RAW):
                    sp.wait_ge(w1_T, RAW * m + (c - RAW + 1))
                    load_w1(m * (RAW * P) + c * P, c)
                    sp.wait_ge(w2_ready, RAW * m + (c - RAW + 1))
                    sp.dma_start(w2_raw[:, c, :], w2_rows[ds(m * (RAW * P) + c * P, P), :]).then_inc(w2_in[c], 16)

        @block.gpsimd
        def _(pool):
            chain = [0]

            def link(ins):
                chain[0] += 1
                ins.then_inc(pool_chain, 1)
                pool.wait_ge(pool_chain, chain[0])

            link(pool.memset(ident[:, :], 0.0))
            pool.affine_select(out=ident[:, :], in_=ident[:, :], compare_op=ALU.not_equal, fill=1.0, base=0,
                               pattern=[[-1, P]], channel_multiplier=1).then_inc(consts_ready, 1)
            link(pool.memset(sign[:, :, :, :], 1.0))
            NEGATIVE = (((0, 1), (0, 2), (0, 3), (1, 2), (2, 3), (3, 1)), ((1, 0), (1, 2), (2, 0), (2, 3), (3, 0), (3, 1)))
            for a in range(2):
                for i, j in NEGATIVE[a]:
                    ins = pool.memset(sign[:, a, i, j:j + 1], -1.0)
            ins.then_inc(signs_ready, 1)
            pool.iota(part_i[:, :], pattern=[[0, 1]], base=0, channel_multiplier=1)
            pool.iota(j1[:, :], pattern=[[1, TJ]], base=1, channel_multiplier=0, allow_small_or_imprecise_dtypes=True)
            pool.iota(first_i[:, :], pattern=[[-1, E]], base=E, channel_multiplier=0)
            pool.iota(expert_i[:, :], pattern=[[1, E], [0, BLOCKS // E]], base=0, channel_multiplier=0)
            pool.iota(base_i[:, :], pattern=[[CAP, E]], base=0, channel_multiplier=0).then_inc(consts_ready, 1)
            pool.iota(value[:, :, :], pattern=[[1, P], [0, TJ]], base=0, channel_multiplier=0,
                      allow_small_or_imprecise_dtypes=True)
            link(pool.memset(ones[:, :], 1.0))
            link(pool.memset(carry[:, :, :], 1.0))
            pool.memset(carry[:, :, 0:1], 0.0)
            pool.affine_select(out=before[:, :], in_=ones[:, :], compare_op=ALU.is_gt, fill=0.0, base=0,
                               pattern=[[1, P]], channel_multiplier=-1).then_inc(consts_ready, 1)

            pool.wait_ge(slots_ready, 1)
            for b in range(SB):
                pool.indirect_dma_start(
                    rows[:, b, :], None, x_rows,
                    bass.IndirectOffsetOnAxis(ap=gather_row[:, b:b + 1], axis=0)).then_inc(x0_in[b], 16)
            pool.wait_ge(gates_ready, 1)
            pool.dma_start(gates_dram.rearrange("(p j e) a -> p j (e a)", j=TJ, e=E), gm[:, :, :]).then_inc(gates_stored, 16)
            pool.wait_ge(tables_ready, 1)

            def take_gather(s, par):
                pool.tensor_copy(gather_now[:, par, :], gather_row[:, ds(SB * s, SB)]).then_inc(gather_taken, 1)
                pool.wait_ge(gather_taken, s + 1)
                pool.nop(nofuse=True)

            def take_scatter(s, par):
                pool.tensor_copy(scatter_now[:, par, :], scatter_row[:, ds(SB * s, SB)]).then_inc(scatter_taken, 1)
                pool.tensor_copy(gate_at_now[:, par, :], gate_row[:, ds(SB * s, SB)]).then_inc(scatter_taken, 1)
                pool.wait_ge(scatter_taken, 2 * (s + 1))
                pool.nop(nofuse=True)

            def gather_x(s, par, u, first=False):
                if not first:
                    pool.wait_ge(cut_T, 2 * (2 * s + u - 1))
                    pool.nop(nofuse=True)
                for bb in range(2):
                    b = 2 * u + bb
                    pool.indirect_dma_start(
                        x_blk[:, bb, :], None, x_rows,
                        bass.IndirectOffsetOnAxis(ap=gather_now[:, par, b:b + 1], axis=0)).then_inc(blk_in[bb], 16)

            def gather_rows(par):
                for b in range(SB):
                    pool.indirect_dma_start(
                        rows[:, b, :], None, out_rows,
                        bass.IndirectOffsetOnAxis(ap=gather_now[:, par, b:b + 1], axis=0)).then_inc(rows_in, 16)
                    pool.indirect_dma_start(
                        gate_now[:, b:b + 1], None, gates_dram,
                        bass.IndirectOffsetOnAxis(ap=gate_at_now[:, par, b:b + 1], axis=0)).then_inc(rows_in, 16)

            for s in range(2):
                take_gather(s, s)
                take_scatter(s, s)
            gather_x(1, 1, 0, first=True)
            pool.dma_start(b2_bc[:, :], b2_rows[0:1, :].partition_broadcast(P)).then_inc(b2_in, 16)
            pool.wait_ge(gates_stored, 16)
            pool.wait_ge(out_init, 16 * CHUNKS)
            pool.wait_ge(x_T, SB)
            gather_rows(0)
            gather_x(1, 1, 1)

            def expert(e, last):
                for half in range(SLABS):
                    s = e * SLABS + half
                    end = last and half == SLABS - 1
                    if not (last and half >= SLABS - 2):
                        pool.wait_ge(rows_in, (s + 1) * (32 * SB))
                        pool.nop(nofuse=True)
                        take_gather(s + 2, half)
                        gather_x(s + 2, half, 0)
                    for b in range(SB):
                        pool.wait_ge(sums_ready, SB * (s + 1) + b + 1)
                        pool.nop(nofuse=True)
                        pool.indirect_dma_start(
                            out_rows, bass.IndirectOffsetOnAxis(ap=scatter_now[:, half, b:b + 1], axis=0),
                            rows[:, b, :], None, bounds_check=TOKENS - 1, oob_is_err=False).then_inc(rows_out, 16)
                    pool.wait_ge(rows_out, (s + 1) * (16 * SB))
                    pool.nop(nofuse=True)
                    if not (last and half >= SLABS - 2):
                        take_scatter(s + 2, half)
                    if not end:
                        if half == SLABS - 1:
                            pool.dma_start(b2_bc[:, :], b2_rows[ds(e + 1, 1), :].partition_broadcast(P)
                                           ).then_inc(b2_in, 16)
                        gather_rows((half + 1) % 2)
                    if not (last and half >= SLABS - 2):
                        gather_x(s + 2, half, 1)

            experts(pool, expert)

        @block.scalar
        def _(act):
            act.wait_ge(squares_ready, 1)
            act.activation(nrm[:, 2:4], nrm[:, 0:2], ACT.Sqrt).then_inc(norms_ready, 1)

            def keep_logits(g):
                act.wait_ge(xT_used, Q * (g + 1))
                if g >= 2:
                    act.wait_ge(logits_T, g - 1)
                act.activation(logitsT[:, g % 2, :], hp[0:2 * E, g % 2, :], ACT.Copy).then_inc(logitsT_kept, 1)

            for u in range(UNITS):
                act.wait_ge(xT_ps, u + 1)
                if u >= XBUF:
                    act.wait_ge(xT_used, u - XBUF + 1)
                act.activation(xT_hi[:, u % XBUF, :], eo[:, u % Q, :], ACT.Copy).then_inc(xT_hi_ready, 1)
                if u % Q == Q - 1 and u >= Q:
                    keep_logits(u // Q - 1)
            keep_logits(CHUNKS - 1)
            act.wait_ge(shifted, 1)
            act.activation(ex[:, :, :], dl[:, :, :], ACT.Exp).then_inc(exps_ready, 1)
            act.wait_ge(consts_ready, 2)
            act.wait_ge(part_ready, 1)
            for c in range(2 * TOPK):
                k, js = c // 2, slice(c % 2 * JH, (c % 2 + 1) * JH)
                act.wait_ge(hot_t_ready, c + 1)
                act.activation(hot_q[:, k, 1, :, js], hot_t[:, c % 2, :, :], ACT.Copy, scale=part_f[:, :]
                               ).then_inc(hots_p_ready, 1)
            act.wait_ge(slots_ready, 1)
            act.wait_ge(out_init, 16 * CHUNKS)

            def make_tile(e, hh, n, c):
                act.wait_ge(w1_T, n + 1)
                act.activation(w1T_hi[:, hh, :, :], w1_turned[:, c, :, :], ACT.Copy).then_inc(w1_hi_ready, 1)
                act.wait_ge(w2_in[c], 16 * e * (HT // RAW) + 16 * (hh // RAW + 1))
                act.activation(w2_hi[:, hh, :], w2_raw[:, c, :], ACT.Copy).then_inc(w2_hi_ready, 1)

            def hidden(g, hh, prior=True):
                c = hh % 2
                act.wait_ge(fc1_done, g + 1)
                if prior:
                    act.wait_ge(fc2_done, g * SB)
                act.activation(h_hi[:, c, :], hp[:, c, :], ACT.Relu, bias=b1_now[:, hh:hh + 1]).then_inc(h_hi_ready, 1)
                if prior:
                    act.wait_ge(h_ready, g + 1)
                act.activation(h_full[:, :], hp[:, c, :], ACT.Relu, bias=b1_now[:, hh:hh + 1]).then_inc(h_full_ready, 1)

            def split_y(s, par, u):
                act.wait_ge(rotated, 8 * s + 4 * u + (4 - 8 + FIRST))
                act.activation(yT_hi[:, par, :, u * HALF:(u + 1) * HALF], y_half[:, :, :], ACT.Copy
                               ).then_inc(y_hi_ready, 1)

            for n in range(AHEAD):
                make_tile(0, n, n, n)
            for u, y in enumerate((y_half, y_half2)):
                act.wait_ge(x_T, 2 * (u + 1))
                for i in range(Q):
                    act.activation(y[:, i, :], eo_half[:, 4 * u, :], ACT.Copy, scale=rot[:, i, 0:1]).then_inc(y0_begun, 1)
            for u, y in enumerate((y_half, y_half2)):
                act.wait_ge(rotated, 3 * (u + 1))
                act.activation(yT_hi[:, 0, :, u * HALF:(u + 1) * HALF], y[:, :, :], ACT.Copy).then_inc(y_hi_ready, 1)
            act.wait_ge(b1_kept, 1)
            act.activation(b1_now[:, :], b1T[:, 0:HT], ACT.Copy).then_inc(b1_taken, 1)
            act.wait_ge(b1_taken, 1)
            hidden(0, 0, prior=False)

            def expert(e, last):
                for half in range(SLABS):
                    for hh in range(HT):
                        end = last and half == SLABS - 1
                        g = e * STEPS + half * HT + hh
                        if half == 0 and hh + AHEAD < HT:
                            make_tile(e, hh + AHEAD, e * HT + hh + AHEAD, hh % RAW)
                        if half == SLABS - 1 and hh + AHEAD >= HT and not last:
                            make_tile(e + 1, hh + AHEAD - HT, e * HT + hh + AHEAD, hh % RAW)
                        if not (end and hh == HT - 1):
                            if hh == HT - 1 and half == SLABS - 1:
                                act.wait_ge(b1_found, e + 1)
                                act.wait_ge(h_full_ready, g + 1)
                                act.activation(b1_now[:, :], b1_next[:, :], ACT.Copy).then_inc(b1_taken, 1)
                                act.wait_ge(b1_taken, e + 2)
                            hidden(g + 1, (hh + 1) % HT)
                        if half == SLABS - 1 and hh == HT // 2 and not last:
                            act.activation(b1_next[:, :], b1T[:, ds((e + 1) * HT, HT)], ACT.Copy).then_inc(b1_found, 1)
                        if not end:
                            s1 = e * SLABS + half + 1
                            if hh in STORE_AT:
                                u = STORE_AT.index(hh)
                                for bb in range(2):
                                    act.wait_ge(blk_in[bb], 16 * (2 * s1 + u - 1))
                                act.dma_start(slots_dram[u].rearrange("b p d -> p b d"), x_blk[:, :, :]).then_inc(cut_out, 16)
                            for u in range(2):
                                if hh == CUT_AT[u]:
                                    act.wait_ge(cut_out, 16 * (2 * s1 + u - 1))
                                if CUT_AT[u] <= hh < CUT_AT[u] + 3:
                                    for n in CUT_PARTS[hh - CUT_AT[u]]:
                                        bb, dq = n // CUT_DMAS, n % CUT_DMAS
                                        load_cut(act, x_blk[:, bb, :], slots_dram[u, bb], cut_in, parts=(dq,))
                            if hh in HI_AT:
                                split_y(s1, (half + 1) % 2, HI_AT.index(hh))

            experts(act, expert)

        @block.vector
        def _(dve):
            chain = [0]

            def link(ins):
                chain[0] += 1
                ins.then_inc(dve_chain, 1)
                dve.wait_ge(dve_chain, chain[0])

            dve.wait_ge(small_T, 1)
            dve.tensor_copy(gwT[:, :, :].rearrange("p q e -> p (q e)"), gw_ps)
            link(dve.tensor_copy(qq[:, :], small_ps))
            link(dve.tensor_tensor(sq[:, :, :].rearrange("p a q -> p (a q)"), qq[:, 0:2 * Q], qq[:, 0:2 * Q], ALU.mult))
            link(dve.tensor_reduce(nrm[:, 0:2], sq[:, :, :], X, ALU.add))
            dve.tensor_scalar(nrm[:, 0:2], nrm[:, 0:2], 1e-8, None, ALU.add).then_inc(squares_ready, 1)
            dve.wait_ge(norms_ready, 1)
            link(dve.reciprocal(nrm[:, 0:2], nrm[:, 2:4]))
            for a in range(2):
                lastop = dve.tensor_scalar(qn[:, a, :], qq[:, a * Q:(a + 1) * Q], nrm[:, a:a + 1], None, ALU.mult)
            link(lastop)
            MOVES = ((0, slice(0, 4), slice(0, 4)), (1, slice(0, 4, 2), slice(1, 4, 2)), (1, slice(1, 4, 2), slice(0, 4, 2)),
                     (2, slice(0, 2), slice(2, 4)), (2, slice(2, 4), slice(0, 2)), (3, slice(0, 1), slice(3, 4)),
                     (3, slice(1, 2), slice(2, 3)), (3, slice(2, 3), slice(1, 2)), (3, slice(3, 4), slice(0, 1)))
            for i, to, k in MOVES:
                lastop = dve.tensor_copy(spread[:, :, i, to], qn[:, :, k])
            link(lastop)
            dve.wait_ge(signs_ready, 1)
            dve.tensor_tensor(factor[:, 0, :, :], spread[:, 0, :, :], sign[:, 0, :, :], ALU.mult)
            link(dve.scalar_tensor_tensor(factor[:, 1, :, :], spread[:, 1, :, :], qq[:, 2 * Q:2 * Q + 1], sign[:, 1, :, :],
                                          ALU.mult, ALU.mult))
            link(dve.tensor_tensor(rot_terms[:, :, :, :], factor[:, 0, :, :].unsqueeze(2).to_broadcast([P, Q, Q, Q]),
                                   factor[:, 1, :, :].rearrange("p m j -> p j m").unsqueeze(1).to_broadcast([P, Q, Q, Q]),
                                   ALU.mult))
            link(dve.reduce_sum(rot[:, :, :], rot_terms[:, :, :, :], X))
            link(dve.tensor_tensor(grot_terms[:, :, :, :],
                                   rot[:, :, :].rearrange("p i j -> p j i").unsqueeze(2).to_broadcast([P, Q, E, Q]),
                                   gwT[:, :, :].rearrange("p i e -> p e i").unsqueeze(1).to_broadcast([P, Q, E, Q]),
                                   ALU.mult))
            link(dve.reduce_sum(grot[:, :, :], grot_terms[:, :, :, :], X))
            link(dve.tensor_copy(grot_hl[:, :, 0:E], grot[:, :, :]))
            dve.tensor_tensor(grot_hl[:, :, E:2 * E], grot[:, :, :], grot_hl[:, :, 0:E].bitcast(F32), ALU.subtract
                              ).then_inc(grot_ready, 1)
            dve.wait_ge(b1_T, 1)
            dve.tensor_copy(b1T[:, :], b1_ps).then_inc(b1_kept, 1)
            dve.wait_ge(consts_ready, 2)
            dve.tensor_copy(part_f[:, :], part_i[:, :]).then_inc(part_ready, 1)
            dve.tensor_copy(first_f[:, :], first_i[:, :]).then_inc(h_ready, 1)
            dve.tensor_copy(expert_f[:, :], expert_i[:, :])
            link(dve.tensor_copy(base_f[:, :], base_i[:, :]))

            for u in range(UNITS):
                dve.wait_ge(xT_hi_ready, u + 1)
                dve.tensor_tensor(xT_lo[:, u % XBUF, :], eo[:, u % Q, :], xT_hi[:, u % XBUF, :].bitcast(F32), ALU.subtract
                                  ).then_inc(xT_ready, 1)

            def per_e(ap):
                return ap.unsqueeze(2).to_broadcast([P, TJ, E])

            mx, sm, v1, v2, w1m, w2m, gs, g1, g2 = (st[:, k, :] for k in range(9))
            hot3 = hot[:, :, :, :].rearrange("p k e j -> p (k e) j")
            dve.wait_ge(logits_T, CHUNKS)
            link(dve.tensor_copy(lg_low[:, :, :], logits_hl[:, :, 1, :]))
            link(dve.tensor_tensor(lg[:, :, :], logits_hl[:, :, 0, :], lg_low[:, :, :], ALU.add))
            link(dve.reduce_max(mx, lg[:, :, :], X))
            dve.tensor_tensor(dl[:, :, :], lg[:, :, :], per_e(mx), ALU.subtract).then_inc(shifted, 1)
            dve.wait_ge(exps_ready, 1)
            link(dve.reduce_sum(sm, ex[:, :, :], X))
            link(dve.reciprocal(sm, sm))
            link(dve.tensor_tensor(score[:, :, :], ex[:, :, :], per_e(sm), ALU.mult))
            first_bc = first_f[:, :].unsqueeze(1).to_broadcast([P, TJ, E])
            for k, (v, w) in enumerate(((v1, w1m), (v2, w2m))):
                hot_k = hot[:, k, :, :].rearrange("p e j -> p j e")
                link(dve.reduce_max(v, score[:, :, :], X))
                link(dve.tensor_tensor(wt[:, :, :], score[:, :, :], per_e(v), ALU.is_equal))
                link(dve.tensor_tensor(wt[:, :, :], wt[:, :, :], first_bc, ALU.mult))
                link(dve.reduce_max(w, wt[:, :, :], X))
                link(dve.tensor_tensor(hot_k, wt[:, :, :], per_e(w), ALU.is_equal))
                if k == 0:
                    link(dve.scalar_tensor_tensor(score[:, :, :], hot_k, -2.0, score[:, :, :], ALU.mult, ALU.add))
            dve.wait_ge(consts_ready, 3)
            link(dve.tensor_tensor_scan(cnt[:, :, :].rearrange("p k j -> p (k j)"),
                                        carry[:, :, :].rearrange("p k j -> p (k j)"),
                                        hot[:, :, :, :].rearrange("p k e j -> p (k e j)"), 0.0, ALU.mult, ALU.add))
            dve.tensor_copy(tot[:, :], cnt[:, :, TJ - 1]).then_inc(counts_ready, 1)
            link(dve.tensor_scalar(base_kj[:, :, :], st[:, 4:6, :], -float(CAP), float(E * CAP), ALU.mult, ALU.add))
            dve.wait_ge(ahead_ready, 1)
            link(dve.tensor_tensor(ahead[:, :].rearrange("p (k e) -> p k e", k=TOPK),
                                   ahead_ps.rearrange("p (k e) -> p k e", k=TOPK),
                                   base_f[:, :].unsqueeze(1).to_broadcast([P, TOPK, E]), ALU.add))
            link(dve.tensor_tensor(cnt[:, :, :], cnt[:, :, :], ahead[:, :].unsqueeze(2).to_broadcast([P, TOPK * E, TJ]),
                                   ALU.add))
            link(dve.tensor_tensor(loc[:, :, :], cnt[:, :, :], hot3, ALU.mult))
            link(dve.reduce_sum(slot1[:, :, :], loc[:, :, :].rearrange("p (k e) j -> p k j e", k=TOPK), X))
            link(dve.tensor_tensor(place[:, :, :], slot1[:, :, :], base_kj[:, :, :], ALU.subtract))
            link(dve.scalar_tensor_tensor(slot1[:, :, :], place[:, :, :], float(CAP), slot1[:, :, :], ALU.is_le, ALU.mult))
            link(dve.tensor_scalar(slot_i[:, :], slot1[:, :, :].rearrange("p k j -> p (k j)"), -1.0, None, ALU.add))
            dve.tensor_scalar(q_i[:, :], slot_i[:, :], 7, None, ALU.arith_shift_right)
            link(dve.tensor_scalar(b_i[:, :], slot_i[:, :], P - 1, None, ALU.bitwise_and))
            dve.tensor_copy(q_f[:, :, :].rearrange("p k j -> p (k j)"), q_i[:, :]).then_inc(sums_ready, SB)
            link(dve.tensor_copy(b_f[:, :, :].rearrange("p k j -> p (k j)"), b_i[:, :]))
            for c in range(2 * TOPK):
                k, js = c // 2, slice(c % 2 * JH, (c % 2 + 1) * JH)
                if c >= 2:
                    dve.wait_ge(hots_p_ready, c - 1)
                    dve.wait_ge(hots_ready, c - 1)
                dve.tensor_tensor(hot_t[:, c % 2, :, :], value[:, 0:BLOCKS, js],
                                  q_f[:, k:k + 1, js].to_broadcast([P, BLOCKS, JH]), ALU.is_equal).then_inc(hot_t_ready, 1)
                dve.tensor_tensor(hot_b[:, k, :, js], value[:, :, js], b_f[:, k:k + 1, js].to_broadcast([P, P, JH]),
                                  ALU.is_equal)
                dve.wait_ge(hot_t_ready, c + 1)
                dve.tensor_tensor(hot_q[:, k, 0, :, js], hot_t[:, c % 2, :, :],
                                  j1[:, js].unsqueeze(1).to_broadcast([P, BLOCKS, JH]), ALU.mult).then_inc(hots_ready, 1)
            link(dve.tensor_tensor(gs, v1, v2, ALU.add))
            link(dve.reciprocal(gs, gs))
            dve.tensor_tensor(g1, v1, gs, ALU.mult)
            link(dve.tensor_tensor(g2, v2, gs, ALU.mult))
            dve.tensor_tensor(gm[:, :, :], hot[:, 0, :, :].rearrange("p e j -> p j e"), per_e(g1), ALU.mult)
            link(dve.tensor_tensor(wt[:, :, :], hot[:, 1, :, :].rearrange("p e j -> p j e"), per_e(g2), ALU.mult))
            dve.tensor_tensor(gm[:, :, :], gm[:, :, :], wt[:, :, :], ALU.add).then_inc(gates_ready, 1)
            dve.wait_ge(hots_used, 2 * TOPK)
            link(dve.tensor_copy(j_part[:, :], token_ps[:, 0, :]))
            link(dve.scalar_tensor_tensor(token1[:, :], token_ps[:, 1, :], float(TJ), j_part[:, :], ALU.mult, ALU.add))
            dve.tensor_scalar(gather_row[:, :], token1[:, :], -1.0, 0.0, ALU.add, ALU.max).then_inc(slots_ready, 1)
            dve.tensor_scalar(gate_f[:, :], token1[:, :], -1.0, 0.0, ALU.add, ALU.max)
            link(dve.tensor_scalar(skip[:, :], token1[:, :], 0.0, float(SKIP), ALU.is_equal, ALU.mult))
            dve.scalar_tensor_tensor(gate_row[:, :], gate_f[:, :], float(E), expert_f[:, :], ALU.mult, ALU.add)
            dve.scalar_tensor_tensor(scatter_row[:, :], token1[:, :], -1.0, skip[:, :], ALU.add, ALU.add
                                     ).then_inc(tables_ready, 1)

            def turn_tile(e, hh, n, c):
                dve.wait_ge(w1_in[c], 16 * CUT_DMAS * (e * (HT // RAW) + (hh // RAW + 1)))
                dve.wait_ge(w1_ready, n - 1)
                dve.transpose(w1_turned[:, c, :, :].rearrange("p q n -> p (q n)"), w1_raw[:, c, :]).then_inc(w1_T, 1)

            def make_tile(hh, n, c):
                dve.wait_ge(w1_hi_ready, n + 1)
                dve.tensor_tensor(w1T_lo[:, hh, :, :], w1_turned[:, c, :, :], w1T_hi[:, hh, :, :].bitcast(F32), ALU.subtract
                                  ).then_inc(w1_ready, 1)
                dve.wait_ge(w2_hi_ready, n + 1)
                dve.tensor_tensor(w2_lo[:, hh, :], w2_raw[:, c, :], w2_hi[:, hh, :].bitcast(F32), ALU.subtract
                                  ).then_inc(w2_ready, 1)

            def hidden_low(g, c):
                dve.wait_ge(h_full_ready, g + 1)
                dve.tensor_tensor(h_lo[:, c, :], h_full[:, :], h_hi[:, c, :].bitcast(F32), ALU.subtract
                                  ).then_inc(h_ready, 1)

            def turn_x(s, u):
                dve.wait_ge(cut_in, 2 * CUT_DMAS * 16 * (2 * s + u - 1))
                dve.wait_ge(rotated, 8 * s + 4 * u + (FIRST - 8))
                for bb in range(2):
                    dve.transpose(x_turned[:, bb, :, :].rearrange("p q n -> p (q n)"), x_blk[:, bb, :]
                                  ).then_inc(cut_T, 1)

            def rotate(s, u, j):
                if j == 0:
                    dve.wait_ge(cut_T, 2 * (2 * s + u))
                    dve.wait_ge(y_ready, 2 * s + u)
                else:
                    dve.wait_ge(rotated, 8 * s + 4 * u + (j - 8 + FIRST))
                for i in range(Q):
                    y = y_half[:, i, :].rearrange("p (b n) -> p b n", b=2)
                    if j == 0:
                        ins = dve.tensor_scalar(y, x_turned[:, :, j, :], rot[:, i, j:j + 1], None, ALU.mult)
                    else:
                        ins = dve.scalar_tensor_tensor(y, x_turned[:, :, j, :], rot[:, i, j:j + 1], y, ALU.mult, ALU.add)
                ins.then_inc(rotated, 1)

            def split_y(s, par, u, y=y_half):
                dve.wait_ge(y_hi_ready, 2 * s + u + 1)
                dst = slice(u * HALF, (u + 1) * HALF)
                dve.tensor_tensor(yT_lo[:, par, :, dst], y[:, :, :], yT_hi[:, par, :, dst].bitcast(F32),
                                  ALU.subtract).then_inc(y_ready, 1)

            for n in range(AHEAD):
                dve.wait_ge(w1_in[n], 16 * CUT_DMAS)
                dve.transpose(w1_turned[:, n, :, :].rearrange("p q n -> p (q n)"), w1_raw[:, n, :]).then_inc(w1_T, 1)
                make_tile(n, n, n)
            def add_component(u, y, j, n):
                if n:
                    dve.wait_ge(rotated, 3 * u + n)
                for i in range(Q):
                    if n == 0:
                        dve.wait_ge(y0_begun, Q * u + i + 1)
                    ins = dve.scalar_tensor_tensor(y[:, i, :], eo_half[:, 4 * u + j, :], rot[:, i, j:j + 1], y[:, i, :],
                                                   ALU.mult, ALU.add)
                ins.then_inc(rotated, 1)

            dve.nop().then_inc(cut_T, 2)
            add_component(0, y_half, 2, 0)
            add_component(0, y_half, 3, 1)
            add_component(0, y_half, 1, 2)
            add_component(1, y_half2, 2, 0)
            split_y(0, 0, 0)
            add_component(1, y_half2, 3, 1)
            add_component(1, y_half2, 1, 2)
            split_y(0, 0, 1, y_half2)
            hidden_low(0, 0)

            def expert(e, last):
                for half in range(SLABS):
                    s = e * SLABS + half
                    end = last and half == SLABS - 1
                    for hh in range(HT):
                        g = e * STEPS + half * HT + hh
                        tile = e * HT + hh + AHEAD
                        if half == 0 and hh + AHEAD < HT:
                            turn_tile(e, hh + AHEAD, tile, hh % RAW)
                            make_tile(hh + AHEAD, tile, hh % RAW)
                        if half == SLABS - 1 and hh + AHEAD >= HT and not last:
                            turn_tile(e + 1, hh + AHEAD - HT, tile, hh % RAW)
                            make_tile(hh + AHEAD - HT, tile, hh % RAW)
                        if not end:
                            if hh == LO_AT[1]:
                                split_y(s + 1, (half + 1) % 2, 1)
                            for u in range(2):
                                if hh == TURN_AT[u]:
                                    turn_x(s + 1, u)
                                if ROT_AT[u] <= hh < ROT_AT[u] + Q:
                                    rotate(s + 1, u, hh - ROT_AT[u])
                        if hh in PRE_AT:
                            b = PRE_AT.index(hh)
                            if b == 0:
                                dve.wait_ge(rows_in, (s + 1) * (32 * SB))
                                dve.wait_ge(b2_in, 16 * (e + 1))
                            dve.scalar_tensor_tensor(rows[:, b, :], b2_bc[:, :], gate_now[:, b:b + 1], rows[:, b, :],
                                                     ALU.mult, ALU.add).then_inc(pre_done, 1)
                        if not (end and hh == HT - 1):
                            hidden_low(g + 1, (hh + 1) % 2)
                        if hh == LO_AT[0] and not end:
                            split_y(s + 1, (half + 1) % 2, 0)
                        if hh == HT - 1:
                            for b in range(SB):
                                dve.wait_ge(fc2_done, (g + 1) * SB + b + 1)
                                dve.wait_ge(pre_done, SB * s + b + 1)
                                dve.scalar_tensor_tensor(rows[:, b, :], eo[:, b, :], gate_now[:, b:b + 1],
                                                         rows[:, b, :], ALU.mult, ALU.add).then_inc(sums_ready, 1)

            experts(dve, expert)

        @block.tensor
        def _(pe):
            pe.wait_ge(consts_ready, 1)
            pe.wait_ge(small_in, 48)
            pe.wait_ge(gw_in, 16)
            pe.transpose(small_ps, small[0:9, :], ident[0:9, 0:9]).then_inc(fc2_done, SB)
            for q in range(Q):
                ins = pe.transpose(gw_ps[:, q * E:(q + 1) * E], gw_nat[:, q * P:(q + 1) * P], ident[0:E, 0:E])
            ins.then_inc(small_T, 1)

            def take_logits(u):
                bank = hp[0:2 * E, (u // Q) % 2, :]
                q = u % Q
                pe.wait_ge(xT_ready, u + 1)
                if q == 0 and u >= 2 * Q:
                    pe.wait_ge(logitsT_kept, u // Q - 1)
                pe.matmul(bank, grot_hl[:, q, :], xT_hi[:, u % XBUF, :], start=(q == 0), stop=False)
                pe.matmul(bank, grot_hl[:, q, :], xT_lo[:, u % XBUF, :], start=False, stop=(q == Q - 1)).then_inc(xT_used, 1)

            def turn_logits(g):
                pe.wait_ge(logitsT_kept, g + 1)
                for t in range(XC):
                    at = (g * XC + t) * 2 * E
                    ins = pe.transpose(logits_bank[:, at:at + 2 * E], logitsT[:, g % 2, t * P:(t + 1) * P],
                                       ident[0:2 * E, 0:2 * E])
                ins.then_inc(logits_T, 1)

            for u in range(UNITS + LAG):
                if u < UNITS:
                    if u < Q:
                        pe.wait_ge(x_in0[u], 16)
                    elif u % Q == 0:
                        pe.wait_ge(x_in[u // Q][0], 16)
                    for t in range(XC):
                        ins = pe.transpose(eo[:, u % Q, t * P:(t + 1) * P],
                                           x_all[:, (u // Q) * XC + t, (u % Q) * P:(u % Q + 1) * P], ident[:, :])
                    ins.then_inc(xT_ps, 1)
                if u == LAG - 1:
                    pe.wait_ge(b1_in, 16)
                    pe.wait_ge(grot_ready, 1)
                    pe.transpose(b1_ps, b1_nat[:, :], ident[:, :]).then_inc(b1_T, 1)
                if u >= LAG:
                    take_logits(u - LAG)
                if u % Q == 1 and u >= 2 * Q:
                    turn_logits(u // Q - 2)
            turn_logits(CHUNKS - 1)

            pe.wait_ge(consts_ready, 3)
            pe.wait_ge(counts_ready, 1)
            pe.matmul(ahead_ps, before[:, :], tot[:, :], start=True, stop=False)
            pe.matmul(ahead_ps[:, E:2 * E], ones[:, :], tot[:, 0:E], start=False, stop=True).then_inc(ahead_ready, 1)

            def fc1(g, tile, hh, par):
                pe.wait_ge(w1_ready, tile + 1)
                pe.wait_ge(h_ready, g)
                bank = hp[:, hh % 2, :]
                for q in range(Q):
                    pe.matmul(bank, w1T_hi[:, hh, q, :], yT_hi[:, par, q, :], start=(q == 0), stop=False)
                    pe.matmul(bank, w1T_hi[:, hh, q, :], yT_lo[:, par, q, :], start=False, stop=False)
                    ins = pe.matmul(bank, w1T_lo[:, hh, q, :], yT_hi[:, par, q, :], start=False, stop=(q == Q - 1))
                ins.then_inc(fc1_done, 1)

            def fc2(e, g, s, hh, c):
                pe.wait_ge(w2_ready, e * HT + hh + 1)
                pe.wait_ge(h_hi_ready, g + 1)
                for b in range(SB):
                    if hh == 0:
                        pe.wait_ge(sums_ready, SB * s + (b + 1))
                    blk = slice(b * P, (b + 1) * P)
                    pe.matmul(eo[:, b, :], h_hi[:, c, blk], w2_hi[:, hh, :], start=(hh == 0), stop=False)
                    pe.matmul(eo[:, b, :], h_hi[:, c, blk], w2_lo[:, hh, :], start=False, stop=False)
                pe.wait_ge(h_ready, g + 2)
                for b in range(SB):
                    blk = slice(b * P, (b + 1) * P)
                    pe.matmul(eo[:, b, :], h_lo[:, c, blk], w2_hi[:, hh, :], start=False, stop=(hh == HT - 1)
                              ).then_inc(fc2_done, 1)

            for c in range(2 * TOPK):
                pe.wait_ge(hots_ready, c + 1)
                pe.wait_ge(hots_p_ready, c + 1)
                for j in range(c % 2 * JH, (c % 2 + 1) * JH):
                    ins = pe.matmul(token_ps, hot_b[:, c // 2, :, j], hot_q[:, c // 2, :, :, j],
                                    start=(c == 0 and j == 0), stop=(c == 2 * TOPK - 1 and j == TJ - 1))
                ins.then_inc(hots_used, 1)
            for b in range(SB):
                pe.wait_ge(x0_in[b], 16)
                for j in range(Q):
                    ins = pe.transpose(eo_half[:, 4 * (b // 2) + j, b % 2 * P:(b % 2 + 1) * P], rows[:, b, j * P:(j + 1) * P], ident[:, :])
                ins.then_inc(x_T, 1)
            pe.wait_ge(w1_ready, 1)
            for u in range(2):
                pe.wait_ge(y_ready, u + 1)
                cols = slice(u * HALF, (u + 1) * HALF)
                for q in range(Q):
                    pe.matmul(hp[:, 0, cols], w1T_hi[:, 0, q, :], yT_hi[:, 0, q, cols], start=(q == 0), stop=False)
                    pe.matmul(hp[:, 0, cols], w1T_hi[:, 0, q, :], yT_lo[:, 0, q, cols], start=False, stop=False)
                    ins = pe.matmul(hp[:, 0, cols], w1T_lo[:, 0, q, :], yT_hi[:, 0, q, cols], start=False, stop=(q == Q - 1))
            ins.then_inc(fc1_done, 1)

            def expert(e, last):
                for half in range(SLABS):
                    s = e * SLABS + half
                    end = last and half == SLABS - 1
                    for hh in range(HT):
                        g = e * STEPS + half * HT + hh
                        if hh < HT - 1:
                            fc1(g + 1, e * HT + hh + 1, hh + 1, half)
                        elif not end:
                            pe.wait_ge(y_ready, 2 * (s + 2))
                            fc1(g + 1, e * HT + (HT if half == SLABS - 1 else 0), 0, (half + 1) % 2)
                        fc2(e, g, s, hh, hh % 2)

            experts(pe, expert)


_INS = ['x', 'cond_256', 'L0_cond_q_right', 'L0_cond_spectral_gate', 'L0_ffn_gate_w', 'L0_ffn_fc1_w',
        'L0_ffn_fc1_b', 'L0_ffn_fc2_w', 'L0_ffn_fc2_b']


def kernel(**inputs):
    import numpy as _np
    import concourse.bacc as _bacc
    from concourse import mybir as _mybir
    from concourse.bass_utils import run_bass_kernel_spmd as _run

    nc = _bacc.Bacc("TRN2", target_bir_lowering=False, num_devices=1)
    arrays, args = {}, []
    for name in _INS:
        a = _np.ascontiguousarray(inputs[name])
        arrays[f"in_{name}"] = a
        args.append(nc.dram_tensor(f"in_{name}", a.shape, _mybir.dt.from_np(a.dtype), kind="ExternalInput").ap())
    shape = tuple(inputs["x"].shape)
    args.append(nc.dram_tensor("out_0", shape, _mybir.dt.float32, kind="ExternalOutput").ap())
    program(nc, *args)
    r = _run(nc, [arrays], core_ids=[0])
    return r.results[0]["out_0"]
```
